# Optimizing a Trainium2 kernel written in Bass

```python
import numpy as np
import jax
import jax.numpy as jnp

def _softmax(x, axis=-1):
    return jax.nn.softmax(x, axis=axis)

def _gelu(x):
    return jax.nn.gelu(x, approximate=True)

def _silu(x):
    return jax.nn.silu(x)

def _sigmoid(x):
    return jax.nn.sigmoid(x)

def _layernorm(x, axis=-1, eps=1e-05):
    m = jnp.mean(x, axis=axis, keepdims=True)
    v = jnp.var(x, axis=axis, keepdims=True)
    return (x - m) / jnp.sqrt(v + eps)

def _scatter_add(tgt, idx, src, axis=0):
    return tgt.at[idx].add(src)

def _segment_sum(src, seg, n):
    return jax.ops.segment_sum(src, seg, n)
kernel_name = 'mk_adaln_ffn_d2_seqx_r4_c24122'

def setup_inputs(seed: int=0):
    np.random.seed(seed)
    _w = jnp.asarray

    def _rec_inputs():
        import jax
        import jax.numpy as jnp
        _rk = jax.random.key(seed)
        x = -7.109e-05 + 0.9999 * jax.random.normal(jax.random.fold_in(_rk, 1), (32, 64, 1024), jnp.float32)
        _lenS = 64 - jax.random.randint(jax.random.fold_in(_rk, 7), (32,), 0, max(1, 64 // 4) + 1, jnp.int32)
        _lenS2 = 64 - jax.random.randint(jax.random.fold_in(_rk, 8), (32,), 0, max(1, 64 // 4) + 1, jnp.int32)
        itok_B_0_15 = jax.random.randint(jax.random.fold_in(_rk, 11), (32,), 0, 16, jnp.int32)
        itok_B_8_3872 = jax.random.randint(jax.random.fold_in(_rk, 12), (32,), 8, 3873, jnp.int32)
        return (x, itok_B_0_15, itok_B_8_3872)
    x, itok_B_0_15, itok_B_8_3872 = _rec_inputs()

    def _L0_cond_setup():
        import jax, jax.numpy as jnp
        import numpy as np
        B, C, T = (64, 64, 1024)
        S, D = (16, 64)
        key = jax.random.key(seed)
        k1, k2, k3 = jax.random.split(key, 3)
        x = jax.random.normal(k1, (B, C, T), dtype=jnp.float32)
        condition = jax.random.randint(k2, (B,), 0, S, dtype=jnp.int64)
        bound = float(np.sqrt(6.0 / C))
        weights = jax.random.uniform(k3, (S, C, D), dtype=jnp.float32, minval=-bound, maxval=bound)
        return {'x': x, 'condition': condition, 'weights': weights}
    _L0_cond_all = _L0_cond_setup()
    _L0_cond_in = {k: v for k, v in _L0_cond_all.items() if k in ('weights',)}
    del _L0_cond_all

    def _L0_ffn_setup():
        import jax, jax.numpy as jnp
        import numpy as np
        IN_FEATURES = 1024

        def _dequantize(qweight, scale, zero_point):
            N, K_packed = qweight.shape
            groups = K_packed // 3
            p = qweight.reshape(N, groups, 3)
            v0 = p[:, :, 0] & 63
            v1 = p[:, :, 0] >> 6 & 63
            v2 = p[:, :, 1] & 63
            v3 = p[:, :, 2] & 63
            unpacked = jnp.stack([v0, v1, v2, v3], axis=2).reshape(N, groups * 4)
            unpacked = unpacked[:, :IN_FEATURES]
            return (unpacked.astype(jnp.float32) - zero_point) * scale
        key = jax.random.key(seed)
        k1, k2, k3, k4, k5 = jax.random.split(key, 5)
        x = jax.random.normal(k1, (8, 512, 1024), dtype=jnp.float32)
        qweight = jax.random.randint(k2, (1024, 768), 0, 1024, dtype=jnp.int32)
        weight_scale = jax.random.uniform(k3, (1024, 1), dtype=jnp.float32) * 0.02 + 0.001
        weight_zero_point = jax.random.uniform(k4, (1024, 1), dtype=jnp.float32) * 63.0
        bias = jax.random.normal(k5, (1024,), dtype=jnp.float32)
        return {'x': x, 'qweight': qweight, 'weight_scale': weight_scale, 'weight_zero_point': weight_zero_point, 'bias': bias}
    _L0_ffn_all = _L0_ffn_setup()
    _L0_ffn_in = {k: v for k, v in _L0_ffn_all.items() if k in ('qweight', 'weight_scale', 'weight_zero_point', 'bias')}
    del _L0_ffn_all

    def _L1_cond_setup():
        import math
        import jax, jax.numpy as jnp
        import numpy as np
        H, N, B, L = (64, 64, 16, 1024)
        DT_MIN, DT_MAX = (0.001, 0.1)

        def _get_kernel(log_dt, C, log_A_real, A_imag, length):
            Cc = C[..., 0] + 1j * C[..., 1]
            dt = jnp.exp(log_dt)
            A = -jnp.exp(log_A_real) + 1j * A_imag
            dtA = A * dt[:, None]
            P = dtA[:, :, None] * jnp.arange(length, dtype=jnp.float32)
            Cs = Cc * (jnp.exp(dtA) - 1.0) / A
            K = 2.0 * jnp.einsum('hn,hnl->hl', Cs, jnp.exp(P)).real
            return K
        key = jax.random.key(seed)
        ks = jax.random.split(key, 6)
        u = jax.random.normal(ks[0], (B, H, L), dtype=jnp.float32)
        length = jax.random.randint(ks[1], (B,), 0, L)
        log_dt = jax.random.uniform(ks[2], (H,), dtype=jnp.float32) * (math.log(DT_MAX) - math.log(DT_MIN)) + math.log(DT_MIN)
        C = jax.random.normal(ks[3], (H, N, 2), dtype=jnp.float32)
        log_A_real = jnp.log(0.5 * jnp.ones((H, N), dtype=jnp.float32))
        A_imag = math.pi * jnp.broadcast_to(jnp.arange(N, dtype=jnp.float32), (H, N))
        D = jax.random.normal(ks[4], (H,), dtype=jnp.float32)
        return {'u': u, 'length': length, 'log_dt': log_dt, 'C': C, 'log_A_real': log_A_real, 'A_imag': A_imag, 'D': D}
    _L1_cond_all = _L1_cond_setup()
    _L1_cond_in = {k: v for k, v in _L1_cond_all.items() if k in ('log_dt', 'C', 'log_A_real', 'A_imag', 'D')}
    del _L1_cond_all

    def _L1_ffn_setup():
        import jax, jax.numpy as jnp
        import numpy as np
        B_L, B_H = (4, 8)
        LIN_SLOPE, LIN_INTER, EST_T = (1.0, 0.0, 64.0)
        BATCH, SEQ, IN_F, OUT_F = (4, 512, 1024, 1024)
        MAX_BITS = 8

        def dequant_kbit(qweight, lut, bit):
            O, I32 = (qweight.shape[1], qweight.shape[2])
            shifts = jnp.arange(32, dtype=jnp.int32)
            idx = jnp.zeros((O, I32 * 32), dtype=jnp.int32)
            for p in range(bit):
                bits = (qweight[p][:, :, None] >> shifts & 1).reshape(O, I32 * 32)
                idx = idx | bits << p
            return jnp.take_along_axis(lut, idx, axis=1)
        key = jax.random.key(seed)
        k = jax.random.split(key, 5)
        x = jax.random.normal(k[0], (BATCH, SEQ, IN_F), dtype=jnp.float32)
        qweight = jax.random.randint(k[1], (MAX_BITS, OUT_F, IN_F // 32), 0, 2147483647, dtype=jnp.int32)
        lut4 = jax.random.normal(k[2], (OUT_F, 2 ** B_L), dtype=jnp.float32) * 0.02
        lut8 = jax.random.normal(k[3], (OUT_F, 2 ** B_H), dtype=jnp.float32) * 0.02
        bias = jax.random.normal(k[4], (OUT_F,), dtype=jnp.float32) * 0.01
        return {'x': x, 'qweight': qweight, 'lut4': lut4, 'lut8': lut8, 'bias': bias}
    _L1_ffn_all = _L1_ffn_setup()
    _L1_ffn_in = {k: v for k, v in _L1_ffn_all.items() if k in ('qweight', 'lut4', 'lut8', 'bias')}
    del _L1_ffn_all
    return {'x': x, 'itok_B_0_15': itok_B_0_15, 'itok_B_8_3872': itok_B_8_3872, 'L0_cond_weights': _L0_cond_in['weights'], 'L0_ffn_qweight': _L0_ffn_in['qweight'], 'L0_ffn_weight_scale': _L0_ffn_in['weight_scale'], 'L0_ffn_weight_zero_point': _L0_ffn_in['weight_zero_point'], 'L0_ffn_bias': _L0_ffn_in['bias'], 'L1_cond_log_dt': _L1_cond_in['log_dt'], 'L1_cond_C': _L1_cond_in['C'], 'L1_cond_log_A_real': _L1_cond_in['log_A_real'], 'L1_cond_A_imag': _L1_cond_in['A_imag'], 'L1_cond_D': _L1_cond_in['D'], 'L1_ffn_qweight': _L1_ffn_in['qweight'], 'L1_ffn_lut4': _L1_ffn_in['lut4'], 'L1_ffn_lut8': _L1_ffn_in['lut8'], 'L1_ffn_bias': _L1_ffn_in['bias']}

def reference(x, itok_B_0_15, itok_B_8_3872, L0_cond_weights, L0_ffn_qweight, L0_ffn_weight_scale, L0_ffn_weight_zero_point, L0_ffn_bias, L1_cond_log_dt, L1_cond_C, L1_cond_log_A_real, L1_cond_A_imag, L1_cond_D, L1_ffn_qweight, L1_ffn_lut4, L1_ffn_lut8, L1_ffn_bias):
    import jax
    import jax.numpy as jnp

    def _L0_cond_ref(x, condition, weights):
        import jax, jax.numpy as jnp
        import numpy as np
        B, C, T = (64, 64, 1024)
        S, D = (16, 64)
        W = weights[condition]
        return jnp.einsum('bct,bcd->bdt', x, W)

    def _L0_ffn_ref(x, qweight, weight_scale, weight_zero_point, bias):
        import jax, jax.numpy as jnp
        import numpy as np
        IN_FEATURES = 1024

        def _dequantize(qweight, scale, zero_point):
            N, K_packed = qweight.shape
            groups = K_packed // 3
            p = qweight.reshape(N, groups, 3)
            v0 = p[:, :, 0] & 63
            v1 = p[:, :, 0] >> 6 & 63
            v2 = p[:, :, 1] & 63
            v3 = p[:, :, 2] & 63
            unpacked = jnp.stack([v0, v1, v2, v3], axis=2).reshape(N, groups * 4)
            unpacked = unpacked[:, :IN_FEATURES]
            return (unpacked.astype(jnp.float32) - zero_point) * scale
        w = _dequantize(qweight, weight_scale, weight_zero_point)
        return jnp.einsum('bsk,nk->bsn', x, w) + bias

    def _L1_cond_ref(u, length, log_dt, C, log_A_real, A_imag, D):
        import math
        import jax, jax.numpy as jnp
        import numpy as np
        H, N, B, L = (64, 64, 16, 1024)
        DT_MIN, DT_MAX = (0.001, 0.1)

        def _get_kernel(log_dt, C, log_A_real, A_imag, length):
            Cc = C[..., 0] + 1j * C[..., 1]
            dt = jnp.exp(log_dt)
            A = -jnp.exp(log_A_real) + 1j * A_imag
            dtA = A * dt[:, None]
            P = dtA[:, :, None] * jnp.arange(length, dtype=jnp.float32)
            Cs = Cc * (jnp.exp(dtA) - 1.0) / A
            K = 2.0 * jnp.einsum('hn,hnl->hl', Cs, jnp.exp(P)).real
            return K
        Bq, Hq, Lq = u.shape
        mask = (jnp.arange(Lq) < length[:, None]).astype(u.dtype)
        u_m = u * mask[:, None, :]
        kernel = _get_kernel(log_dt, C, log_A_real, A_imag, Lq)
        n = 2 * Lq
        k_f = jnp.fft.rfft(kernel, n=n)
        u_f = jnp.fft.rfft(u_m, n=n)
        y = jnp.fft.irfft(u_f * k_f, n=n)[..., :Lq]
        y = y + u_m * D[:, None]
        return y * mask[:, None, :]

    def _L1_ffn_ref(x, qweight, lut4, lut8, bias):
        import jax, jax.numpy as jnp
        import numpy as np
        B_L, B_H = (4, 8)
        LIN_SLOPE, LIN_INTER, EST_T = (1.0, 0.0, 64.0)
        BATCH, SEQ, IN_F, OUT_F = (4, 512, 1024, 1024)
        MAX_BITS = 8

        def dequant_kbit(qweight, lut, bit):
            O, I32 = (qweight.shape[1], qweight.shape[2])
            shifts = jnp.arange(32, dtype=jnp.int32)
            idx = jnp.zeros((O, I32 * 32), dtype=jnp.int32)
            for p in range(bit):
                bits = (qweight[p][:, :, None] >> shifts & 1).reshape(O, I32 * 32)
                idx = idx | bits << p
            return jnp.take_along_axis(lut, idx, axis=1)
        e = jnp.linalg.norm(x, axis=-1) * LIN_SLOPE + LIN_INTER
        mask = e > EST_T
        w_l = dequant_kbit(qweight, lut4, B_L)
        w_h = dequant_kbit(qweight, lut8, B_H)
        y_l = jnp.einsum('bsi,oi->bso', x, w_l)
        y_h = jnp.einsum('bsi,oi->bso', x, w_h)
        y = jnp.where(mask[..., None], y_h, y_l) + bias
        return y
    x = x + _L0_ffn_ref(_L0_cond_ref(x, itok_B_0_15, L0_cond_weights), L0_ffn_qweight, L0_ffn_weight_scale, L0_ffn_weight_zero_point, L0_ffn_bias)
    x = x + _L1_ffn_ref(_L1_cond_ref(x, itok_B_8_3872, L1_cond_log_dt, L1_cond_C, L1_cond_log_A_real, L1_cond_A_imag, L1_cond_D), L1_ffn_qweight, L1_ffn_lut4, L1_ffn_lut8, L1_ffn_bias)
    return x

_drawn_inputs = setup_inputs


def setup_inputs(seed=0):
    import zlib

    import numpy as np

    out = dict(_drawn_inputs(seed))
    spreads = {'L1_cond_log_A_real': (-0.6931471824645996, 0.2)}
    factors = {'L1_ffn_lut4': 54.821, 'L1_ffn_bias': 200.0}
    for name, (base, spread) in spreads.items():
        noise = np.random.default_rng([zlib.crc32(name.encode()), seed]).standard_normal(out[name].shape)
        drawn = base * np.exp(spread * noise) if base else spread * noise
        out[name] = jnp.asarray(drawn.astype(out[name].dtype))
    for name, factor in factors.items():
        out[name] = (out[name] * factor).astype(out[name].dtype)
    return out
```

```python
import math

import concourse.bass as bass
from concourse import mybir


def adaln_ffn_kernel(nc, x, cond_id, length, cond_w, q0, scale0, zero0, bias0,
                     log_dt, cmat, log_a_real, a_imag, dvec, q1, lut4, lut8, bias1, out):
    F32, F32R, BF16 = mybir.dt.float32, mybir.dt.float32r, mybir.dt.bfloat16
    I32, U16, U8 = mybir.dt.int32, mybir.dt.uint16, mybir.dt.uint8
    ALU, ACT = mybir.AluOpType, mybir.ActivationFunctionType
    ds = bass.ds

    B, C, T = x.shape
    NST = a_imag.shape[1]
    P = 128
    ROWS = B * C
    NR = ROWS // P
    KT = T // P
    GRP = q0.shape[1] // 3
    O = T
    NG = O // 8
    BLK = T // P
    GH = 4
    NGH = C // GH
    CG, NCH = 12, 10
    LAST = NG - CG * NCH
    LW = 17
    TILES = NR + 1
    PAD_ID = 2 * ROWS
    THR = float(2.0 ** 12 + 2.0 ** -11)
    MAGIC = 1.5 * 2.0 ** 23
    TAU = 2.0 * math.pi

    kpad = nc.dram_tensor("kpad", [C, P + T], F32).ap()
    x1_dram = nc.dram_tensor("x1_dram", [ROWS, T], F32).ap()
    xc_dram = nc.dram_tensor("xc_dram", [ROWS, T], F32).ap()
    ids_dram = nc.dram_tensor("ids_dram", [TILES * P, 1], I32).ap()

    used = [(nc.sbuf_base + 31) // 32 * 32]

    def region(nbytes):
        at = used[0]
        used[0] += nbytes
        return at

    def at(name, shape, dt, offset):
        return nc.alloc_sbuf_tensor_at(name, shape, dt, offset=offset)

    r_const = region(6 * 1024)
    r_main = region(64 * 1024)
    r_weights = region(32 * 1024)
    r_work = region(43 * 1024)
    r_table = region(60 * 1024)
    assert used[0] <= nc.sbuf_usable_end, (used[0], nc.sbuf_usable_end)

    def packer(start, size):
        pos = [start]

        def put(name, shape, dt):
            n = 1
            for s in shape[1:]:
                n *= s
            n *= {F32: 4, F32R: 4, I32: 4, BF16: 2, U16: 2, U8: 1}[dt]
            n = (n + 31) // 32 * 32
            t = at(name, shape, dt, pos[0])
            pos[0] += n
            assert pos[0] <= start + size, name
            return t
        return put

    const = packer(r_const, 6 * 1024)
    ident = const("ident", [P, P], F32)
    ident_bf = const("ident_bf", [P, P], BF16)
    plane_id = const("plane_id", [P, 4, P], BF16)
    before = const("before", [P, P], F32)
    ones = const("ones", [P, P], F32)
    mask_t = const("mask_t", [P, BLK, B], F32)
    own_block = const("own_block", [P, 8], BF16)
    chan = const("chan", [P, 1], I32)
    code_mask = const("code_mask", [P, 4], I32)
    len_bc = const("len_bc", [P, B], I32)
    len_p = const("len_p", [P, 1], I32)
    len_pf = const("len_pf", [P, 1], F32)
    last_row = const("last_row", [1, 32], F32)
    gate = const("gate", [1, 1], F32)
    cond_sb = const("cond_sb", [1, B], I32)
    xsum = const("xsum", [P, 2], F32)
    s_sb = const("s_sb", [P, 2], F32)
    norm_new = const("norm_new", [P, 2], F32)
    norm2 = const("norm2", [P, NGH], F32)
    d_sb = const("d_sb", [1, C], F32)
    ids_sb = const("ids_sb", [P, TILES], I32)
    gather_id = const("gather_id", [P, TILES], I32)
    table_off = const("table_off", [1, TILES], I32)

    codes_i = at("codes_i", [P, 8, 4, GRP], I32, r_main)
    codes_b = at("codes_b", [P, 8, 4 * GRP], BF16, r_main + 32 * 1024)
    kt = [at(f"kt{n}", [P, C, 32], F32, r_main + n * 8192) for n in range(8)]
    x1t = at("x1t", [P, C, BLK, B], F32, r_main)
    w1 = at("w1", [P, 2, KT, O], F32, r_main)
    w_lo = at("w_lo", [P, 2, KT, O], F32R, r_main)
    w_hi = at("w_hi", [P, 2, KT, O], F32R, r_table - 4 * 1024)

    q_t = at("q_t", [P, KT, O], F32R, r_weights)
    toep = at("toep", [P, 8, T], F32, r_weights)
    onehot = [at(f"onehot{h}", [P, CG, 8, 64], BF16, r_weights + h * 12288) for h in range(2)]
    ffn = packer(r_weights, 32 * 1024)
    x_hi = [ffn(f"x_hi{u}", [P, T], F32R) for u in range(2)]
    x_lo = [ffn(f"x_lo{u}", [P, T], F32R) for u in range(2)]
    yo = [ffn(f"yo{u}", [P, T], F32) for u in range(2)]
    xg = [ffn(f"xg{u}", [P, T], F32) for u in range(2)]

    LUT_F = LW * NG * 4
    raw0 = at("raw0", [P, 8, 3 * GRP], I32, r_work)
    lut_rest = at("lut_rest", [P, LW, NG], F32, r_work)
    lut_nat = at("lut_nat", [P, 8, 256], F32, r_work)
    lut4_nat = at("lut4_nat", [P, 8, 16], F32, r_work + 8192)
    lut_cols = at("lut_cols", [P, LW, P], F32, r_work + LUT_F)
    lutc = at("lutc", [P, 3, NG, LW], BF16, r_work + 2 * LUT_F)
    after_lutc = r_work + 2 * LUT_F + 3 * NG * LW * 2
    work = packer(after_lutc, r_table - after_lutc)
    nat = [work(f"nat{n}", [C, NST], F32) for n in range(24)]
    nat2 = [work(f"nat2_{n}", [C, 2 * NST], F32) for n in range(4)]
    par = [work(f"par{n}", [P, C], F32) for n in range(4)]
    iota_m = work("iota_m", [P, 32], F32)
    natc = work("natc", [C, NST, 2], F32)
    logs, exps, expo, frac_ = [work(n, [C, NST + 1], F32) for n in ("logs", "exps", "expo", "frac_")]
    expo_i = work("expo_i", [C, NST + 1], I32)
    work = packer(r_work, 2 * LUT_F)
    yt = [work(f"yt{u}", [P, BLK, GH * B], F32) for u in range(2)]
    xr = [work(f"xr{u}", [P, T], F32) for u in range(2)]
    code8 = work("code8", [P, KT, NG], U8)
    packed_at = after_lutc + 23040
    work = packer(after_lutc, 23040)
    mask_row = work("mask_row", [P, T], F32)
    junk_c = work("junk_c", [P, T], BF16)
    plane_words = work("plane_words", [P, 4, 32], I32)
    bits = work("bits", [P, 4, KT * P], BF16)
    rep_words = work("rep_words", [P, 4, 16 * 32], I32)
    work = packer(r_work, 2 * LUT_F)
    bd1 = work("bd1", [P, 3, CG, 8 * LW], BF16)
    x1g = [work("x1g0", [P, T], F32)]
    work = packer(after_lutc, 23040)
    x1g.append(work("x1g1", [P, T], F32))
    bias1_bc = work("bias1_bc", [P, O], F32)
    leaf_mask = [work(f"leaf_mask{u}", [P, 4, CG, 8], U8) for u in range(2)]
    sm = [work(f"sm{n}", [P, NGH], F32) for n in range(8)]
    sc = [work(f"sc{n}", [P, 1], F32) for n in range(3)]
    si = [work(f"si{n}", [P, 1], I32) for n in range(2)]
    slots = work("slots", [P, NGH], I32)
    rowid = work("rowid", [P, NGH], I32)
    elem_f = work("elem_f", [P, NGH], F32)
    tile_at = work("tile_at", [1, TILES], F32)
    pad_ids = work("pad_ids", [TILES, P], I32)
    bd = [work("bd0", [P, 3, CG, 8 * LW], BF16), bd1]

    tiles = packer(r_table, 60 * 1024)
    scale_bc = tiles("scale_bc", [P, O], F32)
    nzs_bc = tiles("nzs_bc", [P, O], F32)
    bias0_bc = tiles("bias0_bc", [P, O], F32)
    ht = [[tiles(f"ht{u}{p}", [P, KT, P], F32R) for p in range(2)] for u in range(2)]
    xt = [tiles(f"xt{u}", [P, T], F32) for u in range(2)]
    xb = [tiles(f"xb{u}", [P, T], F32) for u in range(2)]
    set_up = packer(r_table + 11 * 4096, 8192)
    d_row = set_up("d_row", [1, C, 32], F32)
    x1 = [tiles(f"x1_{u}", [P, T], F32) for u in range(2)]
    prod = tiles("prod", [P, T], F32)
    wbd = tiles("wbd", [P, 2, P], F32)
    junk = tiles("junk", [P, T], BF16)
    tab = packer(packed_at, r_table + 60 * 1024 - packed_at)
    packed = tab("packed", [P, NG * 32], I32)
    MC = KT * 4 * CG * 8
    sel = tab("sel", [P, (NCH + 1) * MC], U8)

    ps = nc.alloc_psum_tensor("ps", [P, 8, 512], F32)

    def banks(a, n=2):
        return ps[:, a:a + n, :].rearrange("p a n -> p (a n)")

    def sem(name):
        return nc.alloc_semaphore(name)

    consts = sem("consts")
    ld_small = sem("ld_small")
    ld_q0 = sem("ld_q0")
    ld_bc = sem("ld_bc")
    dve_pre = sem("dve_pre")
    act_pre = sem("act_pre")
    pe_pre = sem("pe_pre")
    qt_mm = sem("qt_mm")
    qt_ev = sem("qt_ev")
    kp_dma = sem("kp_dma")
    kp_zero = sem("kp_zero")
    ld_x = [sem(f"ld_x{u}") for u in range(2)]
    ld_w = [sem(f"ld_w{u}") for u in range(2)]
    xsum_ok = sem("xsum_ok")
    xb_ok = sem("xb_ok")
    h_mm = sem("h_mm")
    h_hi = sem("h_hi")
    h_lo = sem("h_lo")
    main0 = sem("main0")
    x1_ok = sem("x1_ok")
    x1_tr = sem("x1_tr")
    x1t_ok = sem("x1t_ok")
    st_x1 = [sem(f"st_x1{u}") for u in range(2)]
    ld_t = [sem(f"ld_t{n}") for n in range(2 * GH)]
    conv_mm = sem("conv_mm")
    yt_ok = sem("yt_ok")
    row_tr = sem("row_tr")
    xr_ok = sem("xr_ok")
    norm_ok = sem("norm_ok")
    st_xc = [sem(f"st_xc{u}") for u in range(2)]
    ld_words = sem("ld_words")
    ld_rep = sem("ld_rep")
    bits_ok = sem("bits_ok")
    pack_ok = sem("pack_ok")
    code_mm = sem("code_mm")
    code_ok = sem("code_ok")
    sel_ok = sem("sel_ok")
    ld_lut = sem("ld_lut")
    lut_mm = sem("lut_mm")
    lut_hi = sem("lut_hi")
    lut_ok = sem("lut_ok")
    rank = sem("rank")
    rank_mm = sem("rank_mm")
    ids_pad = sem("ids_pad")
    ids_sc = sem("ids_sc")
    ids_ld = sem("ids_ld")
    bd_ok = sem("bd_ok")
    oh_ok = sem("oh_ok")
    leaves = sem("leaves")
    mask_cp = sem("mask_cp")
    picked = sem("picked")
    w_ok = sem("w_ok")
    ld_b1 = sem("ld_b1")
    gat = [sem(f"gat{u}") for u in range(2)]
    gat1 = [sem(f"gat1{u}") for u in range(2)]
    w_hi_ok = sem("w_hi_ok")
    w_lo_ok = sem("w_lo_ok")
    xc_tr = sem("xc_tr")
    x_hi_ok = sem("x_hi_ok")
    x_lo_ok = sem("x_lo_ok")
    res_ok = sem("res_ok")
    main1 = sem("main1")
    yo_ok = sem("yo_ok")
    st_out = [sem(f"st_out{u}") for u in range(2)]

    def pairs(eng, n, step):
        step(0, 0)
        step(1, 1)
        with eng.Fori(1, n // 2 - 1) as i:
            step(2 * i, 0)
            step(2 * i + 1, 1)
        step(n - 2, 0)
        step(n - 1, 1)

    def is_int(v):
        return isinstance(v, int)

    def wait_pos(eng, s, v):
        if not is_int(v) or v > 0:
            eng.wait_ge(s, v)

    def group_rows(dram, g, hh):
        return dram.rearrange("(b c) t -> c b t", c=C)[ds(GH * g + hh, 1), :, :].rearrange("a b t -> (a b) t")

    block = nc.Block()
    with block:

        @block.sync
        def _(sp):
            sp.dma_start(logs[:, NST:], log_dt.rearrange("(c a) -> c a", a=1)).then_inc(ld_small, 16)
            sp.dma_start(natc[:], cmat).then_inc(ld_small, 16)
            sp.dma_start(logs[:, 0:NST], log_a_real).then_inc(ld_small, 16)
            sp.dma_start(nat[1][:], a_imag).then_inc(ld_small, 16)
            sp.dma_start(d_sb[:], dvec.rearrange("(a c) -> a c", a=1)).then_inc(ld_small, 16)
            sp.dma_start(cond_sb[:], cond_id.rearrange("(a c) -> a c", a=1)).then_inc(ld_small, 16)
            sp.dma_start(len_bc[:], bass.AP(tensor=length.tensor, offset=0, ap=[[0, P], [1, B]])).then_inc(ld_small, 16)
            for q in range(GH):
                sp.dma_start(len_p[q * B:(q + 1) * B, :], length.rearrange("(b a) -> b a", a=1)).then_inc(ld_small, 16)
            sp.dma_start(raw0[:], q0.rearrange("(t p) k -> p t k", p=P)).then_inc(ld_q0, 16)
            sp.dma_start(scale_bc[:], bass.AP(tensor=scale0.tensor, offset=0, ap=[[0, P], [1, O]])).then_inc(ld_bc, 16)
            sp.dma_start(nzs_bc[:], bass.AP(tensor=zero0.tensor, offset=0, ap=[[0, P], [1, O]])).then_inc(ld_bc, 16)
            sp.dma_start(bias0_bc[:], bass.AP(tensor=bias0.tensor, offset=0, ap=[[0, P], [1, O]])).then_inc(ld_bc, 16)

            def load_x(r, u):
                sp.dma_start(xt[u][:], x.rearrange("b c t -> (b c) t")[ds(r * P, P), :]).then_inc(ld_x[u], 16)
                for b2 in range(2):
                    which = sp.value_load(cond_sb[0:1, ds(2 * r + b2, 1)], min_val=0, max_val=cond_w.shape[0] - 1)
                    sp.dma_start(wbd[b2 * C:(b2 + 1) * C, u, b2 * C:(b2 + 1) * C],
                                 cond_w[ds(which, 1), :, :].rearrange("a c d -> (a c) d")).then_inc(ld_w[u], 16)

            sp.wait_ge(ld_small, 16 * (7 + GH))
            sp.wait_ge(consts, 1)
            load_x(0, 0)
            load_x(1, 1)

            sp.wait_ge(dve_pre, 1)
            sp.dma_start(lut_nat[:], lut8.rearrange("(a g) c -> g a c", a=8)).then_inc(ld_lut, 16)
            sp.dma_start(lut4_nat[:], lut4.rearrange("(a g) c -> g a c", a=8)).then_inc(ld_lut, 16)

            sp.wait_ge(act_pre, 4)
            falling = bass.AP(tensor=kpad.tensor, offset=0, ap=[[32, 32], [P + T, C], [1, 32]])
            sp.dma_start(falling, kt[0][0:32, :, :]).then_inc(kp_dma, 16)

            def layer0(r, u):
                if not is_int(r) or r < NR - 2:
                    sp.wait_ge(h_mm, r + 1)
                    sp.wait_ge(xb_ok, r + 1)
                    load_x(r + 2, u)
                sp.wait_ge(x1_ok, r + 1)
                sp.dma_start(x1_dram[ds(r * P, P), :], x1[u][:]).then_inc(st_x1[u], 16)

            pairs(sp, NR, layer0)

            def load_toep(g, u):
                for hh in range(GH):
                    if not is_int(g) or g >= 2:
                        sp.wait_ge(conv_mm, GH * (g - 2) + hh + 1)
                    src = kpad[ds(GH * g + hh, 1), :]
                    src = bass.AP(tensor=src.tensor, offset=src.offset, ap=[[1, P], [1, T]])
                    sp.dma_start(toep[:, GH * u + hh, :], src).then_inc(ld_t[GH * u + hh], 16)

            sp.wait_ge(kp_dma, 16)
            sp.wait_ge(kp_zero, 16)
            sp.wait_ge(main0, NR)
            load_toep(0, 0)
            load_toep(1, 1)
            with sp.Fori(1, NGH // 2) as i:
                load_toep(2 * i, 0)
                load_toep(2 * i + 1, 1)

            sp.wait_ge(norm_ok, NGH)
            sp.wait_ge(code_mm, 8)
            sp.dma_start(bias1_bc[:], bass.AP(tensor=bias1.tensor, offset=0, ap=[[0, P], [1, O]])).then_inc(ld_b1, 16)

        @block.gpsimd
        def _(pool):
            g = nc.gpsimd

            def eye(t, base, mult, cmp, fill, src=None):
                g.affine_select(out=t, in_=t, compare_op=cmp, fill=fill, base=base, pattern=[[mult, P]],
                                channel_multiplier=1)

            g.memset(wbd[:], 0.0).then_inc(consts, 1)
            g.memset(d_row[:], 0.0)
            g.memset(last_row[:], 0.0)
            pool.drain()
            g.memset(last_row[:, 31:32], 1.0)
            g.memset(ident[:], 0.0)
            g.memset(ident_bf[:], 0.0)
            g.memset(plane_id[:], 0.0)
            g.memset(ones[:], 1.0)
            g.memset(before[:], 1.0)
            g.memset(own_block[:], 1.0)
            pool.drain()
            eye(ident[:], 0, -1, ALU.not_equal, 1.0)
            eye(ident_bf[:], 0, -1, ALU.not_equal, 1.0)
            for k in range(4):
                eye(plane_id[:, k, :], 0, -1, ALU.not_equal, 2.0 ** (k - 1))
            g.affine_select(out=before[:], in_=before[:], compare_op=ALU.is_ge, fill=0.0, base=-1,
                            pattern=[[1, P]], channel_multiplier=-1)
            g.affine_select(out=own_block[:], in_=own_block[:], compare_op=ALU.is_ge, fill=0.0, base=0,
                            pattern=[[-16, 8]], channel_multiplier=1)
            pool.drain()
            g.affine_select(out=own_block[:], in_=own_block[:], compare_op=ALU.is_ge, fill=0.0, base=15,
                            pattern=[[16, 8]], channel_multiplier=-1)
            g.iota(chan[:], pattern=[[0, 1]], base=0, channel_multiplier=1)
            g.iota(iota_m[:], pattern=[[1, 32]], base=0, channel_multiplier=0, allow_small_or_imprecise_dtypes=True)
            g.iota(mask_t[:].bitcast(I32), pattern=[[P, BLK], [0, B]], base=0, channel_multiplier=1)
            pool.drain()
            g.memset(prod[0:C, 0:P], 0.0).then_inc(consts, 1)
            pool.wait_ge(consts, 2)
            pool.dma_start(kpad[:, T:], prod[0:C, 0:P]).then_inc(kp_zero, 16)

            pool.wait_ge(lut_hi, 4)
            rest = lut_rest[:].rearrange("p l g -> p g l")
            for part in (1, 2):
                g.tensor_tensor(rest, rest, lutc[:, part - 1, :, :], ALU.subtract)
                pool.drain()
                last = g.tensor_copy(lutc[:, part, :, :], rest)
                pool.drain()
            last.then_inc(lut_ok, 1)

            pool.wait_ge(act_pre, 4)
            g.iota(mask_row[:].bitcast(I32), pattern=[[1, T]], base=0, channel_multiplier=0).then_inc(consts, 1)
            pool.wait_ge(ld_bc, 48)

            def layer0(r, u):
                pool.wait_ge(ld_x[u], 8 * (r + 2 - u))
                wait_pos(pool, x1_ok, r - 1)
                g.tensor_tensor(xb[u][:], xt[u][:], bias0_bc[:], ALU.add).then_inc(xb_ok, 1)

            pairs(pool, NR, layer0)

            def load_words(i):
                wait_pos(pool, code_mm, i)
                wait_pos(pool, pack_ok, i)
                pool.dma_start(plane_words[:], q1[4:8, ds(i * P, P), :].rearrange("k g w -> g k w")).then_inc(ld_words, 16)
                for a in range(8):
                    src = q1[0:4, ds(a * P + i * 16, 16), :]
                    src = bass.AP(tensor=src.tensor, offset=src.offset, ap=[[0, 16], [O * 32, 4], [1, 16 * 32]])
                    pool.dma_start(rep_words[16 * a:16 * a + 16, :, :], src).then_inc(ld_rep, 16)

            pool.drain()
            pool.wait_ge(x1_ok, NR)
            load_words(0)
            with pool.Fori(1, 8) as i:
                load_words(i)

            def block_diag(c, u, n):
                if not is_int(c) or c >= 2:
                    pool.wait_ge(leaves, KT * (c - 1))
                for part in range(3):
                    last = g.tensor_tensor(
                        bd[u][:, part, 0:n, :].rearrange("p k (a l) -> p k a l", a=8),
                        lutc[:, part, ds(CG * c, n), :].unsqueeze(2).to_broadcast([P, n, 8, LW]),
                        own_block[:].unsqueeze(1).unsqueeze(3).to_broadcast([P, n, 8, LW]), ALU.mult)
                last.then_inc(bd_ok, 1)

            pool.wait_ge(code_mm, 8)
            pool.wait_ge(pack_ok, 8)
            block_diag(0, 0, CG)

            for q in range(GH):
                g.iota(rowid[q * B:(q + 1) * B, :], pattern=[[GH, NGH]], base=q, channel_multiplier=C)
                pool.drain()
            g.iota(elem_f[:], pattern=[[P, NGH]], base=0, channel_multiplier=1, allow_small_or_imprecise_dtypes=True)
            g.iota(tile_at[:], pattern=[[P, TILES]], base=0, channel_multiplier=0, allow_small_or_imprecise_dtypes=True)
            pool.drain()
            g.memset(pad_ids[:], PAD_ID).then_inc(consts, 1)
            pool.wait_ge(consts, 4)
            pool.dma_start(ids_dram.rearrange("(t p) a -> t (p a)", p=P), pad_ids[:]).then_inc(ids_pad, 16)
            pool.wait_ge(ids_pad, 16)
            pool.wait_ge(norm_ok, NGH)
            for u in range(2):
                pool.wait_ge(st_xc[u], 16 * GH * NGH // 2)
            block_diag(1, 1, CG)
            pool.wait_ge(rank, 3)
            for k in range(NGH):
                pool.indirect_dma_start(ids_dram[:, :], bass.IndirectOffsetOnAxis(ap=slots[:, k:k + 1], axis=0),
                                        rowid[:, k:k + 1], None,
                                        bounds_check=TILES * P - 1, oob_is_err=False).then_inc(ids_sc, 16)

            pool.wait_ge(ids_sc, 16 * NGH)
            pool.dma_start(ids_sb[:], ids_dram.rearrange("(t p) a -> p (t a)", p=P),
                           allow_slow_non_contiguous=True).then_inc(ids_ld, 16)
            with pool.Fori(1, NCH // 2) as i:
                block_diag(2 * i, 0, CG)
                block_diag(2 * i + 1, 1, CG)
            block_diag(NCH, 0, LAST)

            pool.wait_ge(rank, 4)
            pool.wait_ge(ld_b1, 16)

            def gather_xc(k, u):
                pool.indirect_dma_start(xg[u][:], None, xc_dram[:, :],
                                        bass.IndirectOffsetOnAxis(ap=gather_id[:, k:k + 1], axis=0),
                                        bounds_check=ROWS - 1, oob_is_err=False).then_inc(gat[u], 16)

            def gather_x1(k, u):
                pool.indirect_dma_start(x1g[u][:], None, x1_dram[:, :],
                                        bass.IndirectOffsetOnAxis(ap=gather_id[:, k:k + 1], axis=0),
                                        bounds_check=ROWS - 1, oob_is_err=False).then_inc(gat1[u], 16)

            for u in range(2):
                pool.wait_ge(st_x1[u], 16 * NR // 2)
            for k in range(2):
                gather_xc(k, k)
                gather_x1(k, k)
            for k in range(TILES):
                u = k % 2
                if k + 2 < TILES:
                    pool.wait_ge(xc_tr, k + 1)
                    gather_xc(k + 2, u)
                pool.wait_ge(gat1[u], 16 * (k // 2 + 1))
                g.tensor_tensor(x1g[u][:], x1g[u][:], bias1_bc[:], ALU.add).then_inc(res_ok, 1)
                pool.wait_ge(yo_ok, k + 1)
                pool.indirect_dma_start(out.rearrange("b c t -> (b c) t"),
                                        bass.IndirectOffsetOnAxis(ap=ids_sb[:, k:k + 1], axis=0),
                                        yo[u][:], None, bounds_check=ROWS - 1, oob_is_err=False).then_inc(st_out[u], 16)
                if k + 2 < TILES:
                    gather_x1(k + 2, u)
            pool.wait_ge(st_out[0], 16 * ((TILES + 1) // 2))
            pool.wait_ge(st_out[1], 16 * (TILES // 2))

        @block.scalar
        def _(act):
            a = nc.scalar
            (lar, aim, ear, adt, wdt, th, ea, em1, fr, fr2, sn, sh, cm1, cs1, zr, zi, nr_, ni_, m2, tmp,
             tmp2, tmp3, csr, csi) = nat
            act.wait_ge(dve_pre, 2)
            a.activation(ea[:], adt[:], ACT.Exp)
            a.activation(th[:], adt[:], ACT.Tanh, scale=0.5)
            a.activation(sn[:], fr[:], ACT.Sin, scale=TAU)
            a.activation(sh[:], fr2[:], ACT.Sin, scale=TAU).then_inc(act_pre, 1)
            act.wait_ge(dve_pre, 1)
            a.activation(codes_b[:].rearrange("p t k -> p (t k)"), codes_i[:].rearrange("p t v k -> p (t v k)"),
                         ACT.Copy, bias=-32.0).then_inc(act_pre, 1)
            with act.Fori(0, 4) as i:
                for u in range(2):
                    act.wait_ge(qt_mm, 2 * i + u + 1)
                    a.activation(q_t[:, :, ds((2 * i + u) * P, P)],
                                 banks(2 * u).rearrange("p (k n) -> p k n", n=P), ACT.Copy).then_inc(qt_ev, 1)
            act.wait_ge(ld_lut, 32)
            a.activation(lut_cols[:, 0:16, :].rearrange("p h (a l) -> p h a l", l=16),
                         lut_nat[:].rearrange("p a (h l) -> p h a l", l=16), ACT.Copy)
            a.activation(lut_cols[:, 16, :], lut4_nat[:].rearrange("p a l -> p (a l)"), ACT.Copy).then_inc(lut_hi, 1)
            act.drain()
            for n, (first, count) in enumerate(((0, 12), (12, LW - 12))):
                act.wait_ge(lut_mm, n + 1)
                a.activation(lut_rest[:, first:first + count, :].rearrange("p l g -> p (l g)"),
                             banks(5, 3)[:, 0:count * NG], ACT.Copy, scale=0.5).then_inc(lut_hi, 1)
            act.drain()
            a.activation(lutc[:, 0, :, :], lut_rest[:].rearrange("p l g -> p g l"), ACT.Copy).then_inc(lut_hi, 1)

            act.wait_ge(dve_pre, 4)
            a.activation(kt[6][:], kt[0][:], ACT.Exp, scale=32.0)
            a.activation(kt[7][:], kt[0][:], ACT.Exp)
            a.activation(kt[2][:], kt[2][:], ACT.Sin, scale=TAU)
            a.activation(kt[3][:], kt[3][:], ACT.Sin, scale=TAU)
            a.activation(kt[4][:], kt[4][:], ACT.Sin, scale=TAU).then_inc(act_pre, 1)
            act.wait_ge(pe_pre, 2)
            a.activation(kt[0][0:32, :, :], banks(0, 4)[0:32, :].rearrange("p (h m) -> p h m", m=32)[:, :, ::-1], ACT.Copy).then_inc(act_pre, 1)

            def x_sum(r, u):
                act.drain()
                act.wait_ge(ld_x[u], 8 * (r + 2 - u))
                wait_pos(act, h_mm, r - 1)
                a.activation(junk[:], xt[u][:], ACT.Copy, accum_out=xsum[:, u:u + 1]).then_inc(xsum_ok, 1)

            def high_part(r, u):
                act.wait_ge(h_mm, r + 1)
                wait_pos(act, main0, r - 1)
                a.activation(ht[u][0][:].rearrange("p k r -> p (k r)"), banks(0), ACT.Copy).then_inc(h_hi, 1)

            x_sum(0, 0)
            high_part(0, 0)

            def layer0(r, u):
                if not is_int(r) or r < NR - 1:
                    x_sum(r + 1, 1 - u)
                    high_part(r + 1, 1 - u)

            pairs(act, NR, layer0)

            def norms(g, u):
                act.drain()
                act.wait_ge(xr_ok, g + 1)
                for hh in range(GH):
                    act.dma_start(group_rows(xc_dram, g, hh), xr[u][hh * B:(hh + 1) * B, :]).then_inc(st_xc[u], 16)
                a.activation(junk_c[:], xr[u][:], ACT.Square, accum_out=norm_new[:, u:u + 1])
                act.drain()
                a.activation(norm2[:, ds(g, 1)], norm_new[:, u:u + 1], ACT.Copy).then_inc(norm_ok, 1)

            def copy_out(g, u):
                act.wait_ge(conv_mm, GH * (g + 1))
                wait_pos(act, row_tr, g - 1)
                for hh in range(GH):
                    last = a.activation(yt[u][:, :, hh * B:(hh + 1) * B],
                                        banks(2 * u)[:, hh * BLK * B:(hh + 1) * BLK * B].rearrange("p (j b) -> p j b", b=B),
                                        ACT.Copy)
                last.then_inc(yt_ok, 1)
                if not is_int(g) or g > 0:
                    norms(g - 1, 1 - u)

            def codes(i):
                act.wait_ge(code_mm, i + 1)
                wait_pos(act, sel_ok, i)
                a.activation(code8[:].rearrange("p t g -> p (t g)"), banks(6), ACT.Copy).then_inc(code_ok, 1)

            copy_out(0, 0)
            copy_out(1, 1)
            codes(0)
            with act.Fori(1, 8) as i:
                copy_out(2 * i, 0)
                copy_out(2 * i + 1, 1)
                codes(i)
            norms(NGH - 1, 1)

            act.wait_ge(sel_ok, 8)

            def unit(c, uc, n):
                for t in range(KT):
                    u = t % 2
                    wait_pos(act, picked, KT * c + t - 1)
                    a.activation(leaf_mask[u][:].rearrange("p l k a -> p (l k a)")[:, 0:4 * n * 8],
                                 sel[:, ds(c * MC + t * 4 * n * 8, 4 * n * 8)], ACT.Copy).then_inc(mask_cp, 1)
                    if not (is_int(c) and c == 0 and t == 0):
                        store(c if t else c - 1, (t - 1) % KT, n if t else CG)

            def store(c, t, n):
                u = t % 2
                act.wait_ge(picked, KT * c + t + 1)
                view = ps[:, 4 * u:4 * u + 4, 0:n // 4 * 8 * LW].rearrange("p a (k o l) -> p a k o l", o=8, l=LW)
                for l, leaf in ((0, 0), (1, 16)):
                    dst = w1[:, l, t, :].rearrange("p (o g) -> p g o", o=8)[:, ds(CG * c, n), :]
                    last = a.activation(dst.rearrange("p (a k) o -> p a k o", a=4), view[:, :, :, :, leaf], ACT.Copy)
                last.then_inc(w_ok, 1)

            unit(0, 0, CG)
            with act.Fori(1, NCH) as c:
                unit(c, 0, CG)
            unit(NCH, 0, LAST)

            def x_high(k, u):
                act.wait_ge(xc_tr, k + 1)
                wait_pos(act, main1, k - 1)
                a.activation(x_hi[u][:], banks(0), ACT.Copy).then_inc(x_hi_ok, 1)

            x_high(0, 0)
            store(NCH, KT - 1, LAST)
            act.drain()
            for t in range(KT):
                a.activation(w_hi[:, :, t, :], w1[:, :, t, :], ACT.Copy).then_inc(w_hi_ok, 1)
            x_high(1, 1)
            with act.Fori(1, NR // 2) as i:
                x_high(2 * i, 0)
                x_high(2 * i + 1, 1)
            x_high(TILES - 1, 0)

        @block.tensor
        def _(pe):
            mm = nc.tensor.matmul
            pe.wait_ge(act_pre, 2)
            pe.wait_ge(consts, 2)

            def transpose_codes(n, u):
                wait_pos(pe, qt_ev, n - 1)
                for k in range(KT):
                    last = mm(banks(2 * u)[:, k * P:(k + 1) * P],
                              codes_b[:, ds(n, 1), k * P:(k + 1) * P].rearrange("p a k -> p (a k)"),
                              ident_bf[:], start=True, stop=True)
                last.then_inc(qt_mm, 1)

            pairs(pe, 8, transpose_codes)
            pe.wait_ge(dve_pre, 3)
            for n in range(4):
                last = nc.tensor.transpose(ps[:, 4, n * C:(n + 1) * C], nat2[n][:], ident[0:C, 0:C])
            last.then_inc(pe_pre, 1)
            for n, (first, count) in enumerate(((0, 12), (12, LW - 12))):
                pe.wait_ge(lut_hi, n + 1)
                for hi in range(count):
                    last = nc.tensor.transpose(banks(5, 3)[:, hi * P:(hi + 1) * P], lut_cols[:, first + hi, :], ident[:])
                last.then_inc(lut_mm, 1)
            pe.wait_ge(dve_pre, 5)
            pe.wait_ge(qt_ev, 8)
            for h in range(C):
                o = ps[0:32, h // 16, (h % 16) * 32:(h % 16) * 32 + 32]
                mm(o, kt[5][:, h, :], kt[4][:, h, :], start=True, stop=False)
                last = mm(o, last_row[:], d_row[:, h, :], start=False, stop=True)
            last.then_inc(pe_pre, 1)
            pe.wait_ge(act_pre, 4)

            def mix(r, u):
                pe.wait_ge(ld_x[u], 8 * (r + 2 - u))
                pe.wait_ge(ld_w[u], 16 * (r + 2 - u))
                pe.wait_ge(xsum_ok, r + 1)
                for k in range(KT):
                    cols = xt[u][:].rearrange("p (g v) -> p v g", v=4)[:, k // 2, (k % 2) * P:(k % 2) * P + P]
                    mm(banks(0)[:, k * P:(k + 1) * P], cols, wbd[:, u, :], start=True, stop=True)
                mm(ps[:, 6, 0:1], wbd[:, u, :], xsum[:, u:u + 1], start=True, stop=True).then_inc(h_mm, 1)

            def layer0(r, u):
                pe.wait_ge(h_lo, r + 1)
                if not is_int(r) or r < NR - 1:
                    wait_pos(pe, x1t_ok, r - 1)
                    mix(r + 1, 1 - u)
                wait_pos(pe, x1_ok, r - 1)
                for half in range(2):
                    for k in range(KT):
                        for part in range(2):
                            last = mm(ps[:, 2 + 2 * u + half, :], ht[u][part][:, k, :],
                                      q_t[:, k, half * 512:(half + 1) * 512],
                                      start=(k == 0 and part == 0), stop=(k == KT - 1 and part == 1))
                    if half == 0 and (not is_int(r) or r > 0):
                        if not is_int(r) or r < NR - 1:
                            pe.wait_ge(h_lo, r + 2)
                        transpose_x1(r - 1, 1 - u)
                last.then_inc(main0, 1)

            def transpose_x1(r, u):
                pe.wait_ge(x1_ok, r + 1)
                wait_pos(pe, x1t_ok, r)
                for k in range(BLK):
                    last = nc.tensor.transpose(banks(6)[:, k * P:(k + 1) * P], x1[u][:, k * P:(k + 1) * P], ident[:])
                last.then_inc(x1_tr, 1)

            mix(0, 0)
            pairs(pe, NR, layer0)
            transpose_x1(NR - 1, 1)

            pe.wait_ge(x1t_ok, NR)

            def conv(g, u):
                wait_pos(pe, yt_ok, g - 1)
                for hh in range(GH):
                    pe.wait_ge(ld_t[GH * u + hh], 8 * (g + 2 - u))
                    o0 = (hh % 2) * BLK * B
                    for d in range(BLK):
                        rhs = x1t[:, ds(GH * g + hh, 1), 0:BLK - d, :].rearrange("p a k b -> p (a k b)")
                        last = mm(ps[:, 2 * u + hh // 2, o0 + d * B:o0 + BLK * B],
                                  toep[:, GH * u + hh, (BLK - 1 - d) * P:(BLK - d) * P], rhs,
                                  start=(d == 0), stop=(d == BLK - 1))
                    last.then_inc(conv_mm, 1)

            def to_rows(g, u):
                pe.wait_ge(yt_ok, g + 1)
                wait_pos(pe, xr_ok, g)
                for k in range(BLK):
                    last = nc.tensor.transpose(banks(4)[:, k * P:(k + 1) * P], yt[u][:, k, :], ident[:])
                last.then_inc(row_tr, 1)

            def high_codes(i):
                pe.wait_ge(bits_ok, i + 1)
                wait_pos(pe, code_ok, i)
                for t in range(KT):
                    for k in range(4):
                        last = mm(banks(6)[:, t * NG:(t + 1) * NG], bits[:, k, t * P:(t + 1) * P],
                                  plane_id[:, k, :], start=(k == 0), stop=(k == 3))
                last.then_inc(code_mm, 1)

            conv(0, 0)
            conv(1, 1)
            to_rows(0, 0)
            high_codes(0)
            with pe.Fori(1, NGH // 2) as i:
                conv(2 * i, 0)
                to_rows(2 * i - 1, 1)
                conv(2 * i + 1, 1)
                to_rows(2 * i, 0)
                high_codes(i)
            to_rows(NGH - 1, 1)

            pe.wait_ge(yt_ok, NGH)

            def row_ranks():
                pe.wait_ge(xr_ok, NGH)
                pe.wait_ge(rank, 1)
                mm(ps[:, 5, 0:NGH], before[:], sm[0][:], start=True, stop=False)
                mm(ps[:, 5, 0:NGH], ones[:], sm[1][:], start=False, stop=True)
                mm(ps[:, 5, 32:33], ones[:], sc[0][:], start=True, stop=True).then_inc(rank_mm, 1)
                pe.wait_ge(rank, 2)

            def unit(c, uc, n):
                pe.wait_ge(bd_ok, c + 1)
                for t in range(KT):
                    u, half = t % 2, t // 4
                    if t % 4 == 0:
                        pe.wait_ge(oh_ok, 2 * c + half + 1)
                    wait_pos(pe, w_ok, KT * c + t - 1)
                    for k in range(n):
                        lhs = onehot[half][:, k, 2 * (t % 4):2 * (t % 4) + 2, :].rearrange("p j w -> p (j w)")
                        per = n // 4
                        for part in range(3):
                            last = mm(ps[:, 4 * u + k // per, (k % per) * 8 * LW:(k % per + 1) * 8 * LW], lhs,
                                      bd[uc][:, part, k, :], start=(part == 0), stop=(part == 2))
                    last.then_inc(leaves, 1)
                    if is_int(c) and c == 0 and t == 0:
                        row_ranks()
                        pe.wait_ge(code_ok, 8)

            unit(0, 0, CG)
            unit(1, 1, CG)
            with pe.Fori(1, NCH // 2) as i:
                unit(2 * i, 0, CG)
                unit(2 * i + 1, 1, CG)
            unit(NCH, 0, LAST)

            pe.wait_ge(w_ok, KT * (NCH + 1) - 1)
            pe.wait_ge(rank, 4)

            def to_cols(k, u):
                pe.wait_ge(gat[u], 8 * (k + 2 - u))
                wait_pos(pe, x_lo_ok, k)
                for t in range(KT):
                    last = nc.tensor.transpose(banks(0)[:, t * P:(t + 1) * P], xg[u][:, t * P:(t + 1) * P], ident[:])
                last.then_inc(xc_tr, 1)

            def ffn1(k, u):
                if not (is_int(k) and k == TILES - 1):
                    to_cols(k + 1, 1 - u)
                off = pe.value_load(table_off[0:1, ds(k, 1)], min_val=0, max_val=KT * O)
                pe.wait_ge(x_lo_ok, k + 1)
                wait_pos(pe, yo_ok, k - 1)
                hi = w_hi[:].rearrange("p l t o -> p (l t o)")
                lo = w_lo[:].rearrange("p l t o -> p (l t o)")
                for t in range(KT):
                    if is_int(k) and k == 0:
                        pe.wait_ge(w_lo_ok, t + 1)
                    xh, xl = x_hi[u][:, t * P:(t + 1) * P], x_lo[u][:, t * P:(t + 1) * P]
                    for n, (xv, wv) in enumerate(((xh, hi), (xh, lo), (xl, hi))):
                        for half in range(2):
                            last = mm(ps[:, 2 + 2 * u + half, :], xv, wv[:, ds(off + t * O + half * 512, 512)],
                                      start=(t == 0 and n == 0), stop=(t == KT - 1 and n == 2))
                last.then_inc(main1, 1)

            to_cols(0, 0)
            ffn1(0, 0)
            ffn1(1, 1)
            with pe.Fori(1, NR // 2) as i:
                ffn1(2 * i, 0)
                ffn1(2 * i + 1, 1)
            ffn1(TILES - 1, 0)

        @block.vector
        def _(dve):
            v = nc.vector
            tt, ts, stt = v.tensor_tensor, v.tensor_scalar, v.scalar_tensor_tensor
            dve.wait_ge(ld_q0, 16)
            words = raw0[:].rearrange("p t (g k) -> p t k g", k=3)
            ts(codes_i[:, :, 0, :], words[:, :, 0, :], 63, None, ALU.bitwise_and)
            ts(codes_i[:, :, 1, :], words[:, :, 0, :], 6, 63, ALU.logical_shift_right, ALU.bitwise_and)
            ts(codes_i[:, :, 2, :], words[:, :, 1, :], 63, None, ALU.bitwise_and)
            ts(codes_i[:, :, 3, :], words[:, :, 2, :], 63, None, ALU.bitwise_and).then_inc(dve_pre, 1)

            (lar, aim, ear, adt, wdt, th, ea, em1, fr, fr2, sn, sh, cm1, cs1, zr, zi, nr_, ni_, m2, tmp,
             tmp2, tmp3, csr, csi) = nat
            dve.wait_ge(ld_small, 16 * (7 + GH))
            ts(expo[:], logs[:], 1.0 / math.log(2.0), None, ALU.mult)
            dve.drain()
            ts(expo[:], expo[:], MAGIC, MAGIC, ALU.add, ALU.subtract)
            dve.drain()
            stt(frac_[:], expo[:], -0.693359375, logs[:], ALU.mult, ALU.add)
            ts(expo_i[:], expo[:], 127.0, None, ALU.add)
            dve.drain()
            stt(frac_[:], expo[:], 2.12194440e-4, frac_[:], ALU.mult, ALU.add)
            ts(expo_i[:], expo_i[:], 23, None, ALU.logical_shift_left)
            dve.drain()
            ts(exps[:], frac_[:], 1.0 / math.factorial(7), None, ALU.mult)
            for n in range(6, 0, -1):
                dve.drain()
                stt(exps[:], exps[:], 1.0 / math.factorial(n), frac_[:], ALU.add, ALU.mult)
            dve.drain()
            stt(exps[:], exps[:], 1.0, expo_i[:].bitcast(F32), ALU.add, ALU.mult)
            dve.drain()
            ear, dt = exps[:, 0:NST], exps[:, NST:]
            ts(adt[:], ear, dt, -1.0, ALU.mult, ALU.mult)
            ts(wdt[:], aim[:], dt, None, ALU.mult)
            dve.drain()

            def fraction(dst, src, times, t):
                ts(dst, src, times, None, ALU.mult)
                dve.drain()
                ts(t, dst, MAGIC, MAGIC, ALU.add, ALU.subtract)
                dve.drain()
                return tt(dst, dst, t, ALU.subtract)

            fraction(fr[:], wdt[:], 1.0 / TAU, tmp[:])
            dve.drain()
            fraction(fr2[:], wdt[:], 0.5 / TAU, tmp[:]).then_inc(dve_pre, 1)
            dve.wait_ge(act_pre, 1)
            stt(em1[:], ea[:], 1.0, th[:], ALU.add, ALU.mult)
            stt(cm1[:], sh[:], -2.0, sh[:], ALU.mult, ALU.mult)
            tt(zi[:], ea[:], sn[:], ALU.mult)
            dve.drain()
            stt(cs1[:], cm1[:], 1.0, em1[:], ALU.add, ALU.mult)
            dve.drain()
            tt(zr[:], cs1[:], cm1[:], ALU.add)
            dve.drain()
            cr, ci = natc[:, :, 0], natc[:, :, 1]

            def combine(dst, p0, q0_, p1, q1_, op):
                tt(tmp[:], p0, q0_, ALU.mult)
                tt(tmp2[:], p1, q1_, ALU.mult)
                dve.drain()
                tt(dst, tmp[:], tmp2[:], op)
                dve.drain()

            combine(nr_[:], cr, zr[:], ci, zi[:], ALU.subtract)
            combine(ni_[:], cr, zi[:], ci, zr[:], ALU.add)
            combine(m2[:], ear, ear, aim[:], aim[:], ALU.add)
            v.reciprocal(m2[:], m2[:])
            combine(csr[:], ni_[:], aim[:], nr_[:], ear, ALU.subtract)
            combine(csi[:], ni_[:], ear, nr_[:], aim[:], ALU.add)
            alpha, beta, damp, freq = nat2
            stt(alpha[:, 0:NST], csr[:], 2.0, m2[:], ALU.mult, ALU.mult)
            stt(alpha[:, NST:], csi[:], 2.0, m2[:], ALU.mult, ALU.mult)
            stt(beta[:, 0:NST], csi[:], 2.0, m2[:], ALU.mult, ALU.mult)
            stt(beta[:, NST:], csr[:], -2.0, m2[:], ALU.mult, ALU.mult)
            dve.wait_ge(consts, 2)
            v.tensor_copy(d_row[:, :, 0], d_sb[:])
            v.tensor_copy(damp[:, 0:NST], adt[:])
            v.tensor_copy(damp[:, NST:], adt[:])
            ts(freq[:, 0:NST], wdt[:], 1.0 / TAU, None, ALU.mult)
            ts(freq[:, NST:], wdt[:], 1.0 / TAU, None, ALU.mult).then_inc(dve_pre, 1)
            dve.wait_ge(pe_pre, 1)
            for n in range(4):
                v.tensor_copy(par[n][:], ps[:, 4, n * C:(n + 1) * C])
            dve.drain()
            dve.wait_ge(qt_mm, 8)

            def over_m(t):
                return t[:].unsqueeze(2).to_broadcast([P, C, 32])

            m_row = iota_m[:].unsqueeze(1).to_broadcast([P, C, 32])
            tt(kt[0][:], over_m(par[2]), m_row, ALU.mult)
            tt(kt[1][:], over_m(par[3]), m_row, ALU.mult)
            dve.drain()

            def phase(dst, times, shift_lo, shift_hi):
                for lo, sh_ in ((0, shift_lo), (NST, shift_hi)):
                    ts(dst[lo:lo + NST, :, :], kt[1][lo:lo + NST, :, :], times, sh_, ALU.mult, ALU.add)
                dve.drain()
                ts(kt[5][:], dst[:], MAGIC, MAGIC, ALU.add, ALU.subtract)
                dve.drain()
                last = tt(dst[:], dst[:], kt[5][:], ALU.subtract)
                dve.drain()
                return last

            phase(kt[2], 32.0, 0.25, 0.25)
            phase(kt[3], 32.0, 0.0, 0.0)
            phase(kt[4], 1.0, 0.25, 0.0).then_inc(dve_pre, 1)
            dve.wait_ge(act_pre, 3)
            tt(kt[2][:], kt[2][:], over_m(par[0]), ALU.mult)
            tt(kt[3][:], kt[3][:], over_m(par[1]), ALU.mult)
            tt(kt[4][:], kt[4][:], kt[7][:], ALU.mult)
            dve.drain()
            tt(kt[2][:], kt[2][:], kt[3][:], ALU.add)
            dve.drain()
            tt(kt[5][:, :, ::-1], kt[2][:], kt[6][:], ALU.mult).then_inc(dve_pre, 1)

            dve.wait_ge(consts, 2)
            dve.wait_ge(ld_small, 16 * (7 + GH))
            v.tensor_copy(len_pf[:], len_p[:])
            tt(mask_t[:], mask_t[:].bitcast(I32), len_bc[:].unsqueeze(1).to_broadcast([P, BLK, B]), ALU.is_lt)
            for k in range(4):
                ts(code_mask[:, k:k + 1], chan[:], k, 1, ALU.logical_shift_right, ALU.bitwise_and)
            dve.drain()
            ts(code_mask[:], code_mask[:], -1.0, None, ALU.add)
            dve.wait_ge(ld_bc, 48)
            ts(nzs_bc[:], nzs_bc[:], 32.0, -1.0, ALU.subtract, ALU.mult)
            dve.drain()
            tt(nzs_bc[:], nzs_bc[:], scale_bc[:], ALU.mult)
            dve.wait_ge(consts, 3)
            ts(mask_row[:], mask_row[:].bitcast(I32), len_pf[:], None, ALU.is_lt)
            dve.wait_ge(kp_zero, 16)
            dve.wait_ge(kp_dma, 16)
            dve.drain()

            def low_part(r, u):
                dve.wait_ge(h_hi, r + 1)
                v.tensor_copy(s_sb[:, u:u + 1], ps[:, 6, 0:1])
                tt(ht[u][1][:].rearrange("p k r -> p (k r)"), banks(0),
                   ht[u][0][:].rearrange("p k r -> p (k r)").bitcast(F32), ALU.subtract).then_inc(h_lo, 1)

            def layer0(r, u):
                if not is_int(r) or r < NR - 1:
                    low_part(r + 1, 1 - u)
                if not is_int(r) or r > 0:
                    store_x1t(r - 1)
                dve.drain()
                dve.wait_ge(main0, r + 1)
                tt(prod[:], banks(2 + 2 * u), scale_bc[:], ALU.mult)
                dve.drain()
                stt(prod[:], nzs_bc[:], s_sb[:, u:u + 1], prod[:], ALU.mult, ALU.add)
                dve.drain()
                dve.wait_ge(xb_ok, r + 1)
                wait_pos(dve, x1_tr, r - 1)
                if not is_int(r) or r >= 2:
                    dve.wait_ge(st_x1[u], 8 * (r - u))
                tt(x1[u][:], prod[:], xb[u][:], ALU.add).then_inc(x1_ok, 1)

            def store_x1t(r):
                dve.wait_ge(x1_tr, r + 1)
                for b2 in range(2):
                    dst = x1t[:, :, :, ds(2 * r + b2, 1)].rearrange("p h k a -> p k (h a)")
                    src = banks(6).rearrange("p (k b h) -> p k b h", b=2, h=C)[:, :, b2, :]
                    last = tt(dst, src, mask_t[:, :, ds(2 * r + b2, 1)].to_broadcast([P, BLK, C]), ALU.mult)
                last.then_inc(x1t_ok, 1)

            low_part(0, 0)
            pairs(dve, NR, layer0)
            store_x1t(NR - 1)

            def rows(g, u):
                dve.drain()
                dve.wait_ge(row_tr, g + 1)
                wait_pos(dve, norm_ok, g - 1)
                if not is_int(g) or g >= 2:
                    dve.wait_ge(st_xc[u], 32 * (g - u))
                tt(xr[u][:].rearrange("p (j k w) -> p k w j", k=BLK, j=16),
                   banks(4).rearrange("p (k t) -> p k t", t=P)[:, :, ::-1].rearrange("p k (w j) -> p k w j", j=16),
                   mask_row[:].rearrange("p (k w j) -> p k w j", k=BLK, j=16), ALU.mult).then_inc(xr_ok, 1)

            def unpack(dst, src):
                for j in range(16):
                    if j < 15:
                        last = ts(dst(j), src, 14 - j, 0x4000, ALU.logical_shift_left, ALU.bitwise_and)
                    else:
                        last = ts(dst(j), src, 1, 0x4000, ALU.logical_shift_right, ALU.bitwise_and)
                return last

            def plane_bits(i):
                dve.wait_ge(ld_words, 16 * (i + 1))
                wait_pos(dve, code_mm, i)
                bv = bits[:].bitcast(U16).rearrange("p k (j w) -> p k j w", j=16)
                unpack(lambda j: bv[:, :, j, :], plane_words[:].bitcast(U16)).then_inc(bits_ok, 1)

            def pack_onehot(i):
                dve.wait_ge(ld_rep, 128 * (i + 1))
                dst = packed[:, ds(i * 512, 512)]
                ts(dst, rep_words[:, 0, :], code_mask[:, 0:1], None, ALU.bitwise_xor)
                for k in range(1, 4):
                    dve.drain()
                    last = stt(dst, rep_words[:, k, :], code_mask[:, k:k + 1], dst, ALU.bitwise_xor, ALU.bitwise_and)
                last.then_inc(pack_ok, 1)

            def select_masks(i):
                dve.wait_ge(code_ok, i + 1)
                main = sel[:, 0:NCH * MC].rearrange("p (c t l k o) -> p c t l k o", t=KT, l=4, k=CG, o=8)
                tail = sel[:, NCH * MC:NCH * MC + KT * 4 * LAST * 8].rearrange("p (t l k o) -> p t l k o", t=KT, l=4, k=LAST)
                for l in range(4):
                    ts(main[:, :, :, l, :, ds(i, 1)].rearrange("p c t k a -> p t c (k a)"),
                       code8[:, :, 0:NCH * CG].rearrange("p t (c k) -> p t c k", k=CG), 8 >> l, None, ALU.bitwise_and)
                    last = ts(tail[:, :, l, :, ds(i, 1)].rearrange("p t k a -> p t (k a)"),
                              code8[:, :, NCH * CG:], 8 >> l, None, ALU.bitwise_and)
                last.then_inc(sel_ok, 1)

            for u in range(2):
                dve.wait_ge(st_x1[u], 8 * NR)
            plane_bits(0)
            pack_onehot(0)
            rows(0, 0)
            select_masks(0)

            def two_groups(i):
                plane_bits(i)
                pack_onehot(i)
                rows(2 * i - 1, 1)
                rows(2 * i, 0)
                select_masks(i)

            two_groups(1)
            with dve.Fori(2, 8) as i:
                two_groups(i)
            rows(NGH - 1, 1)

            def one_hot(c, half, n):
                wait_pos(dve, leaves, KT * (c - 1) + 4 * half + 4)
                src = packed[:].bitcast(U16).rearrange("p (g w) -> p g w", w=64)[:, ds(CG * c, n), :]
                dst = onehot[half][:].bitcast(U16)
                for jj in range(8):
                    j = 8 * half + jj
                    o = dst[:, 0:n, jj, :]
                    if j < 15:
                        last = ts(o, src, 14 - j, 0x4000, ALU.logical_shift_left, ALU.bitwise_and)
                    else:
                        last = ts(o, src, 1, 0x4000, ALU.logical_shift_right, ALU.bitwise_and)
                last.then_inc(oh_ok, 1)

            def pick(c, t, n):
                u, per = t % 2, n // 4
                dve.wait_ge(leaves, KT * c + t + 1)
                dve.wait_ge(mask_cp, KT * c + t + 1)
                v.memset(gate[:], 0.0)
                view = ps[:, 4 * u:4 * u + 4, 0:per * 8 * LW].rearrange("p a (k l) -> p a k l", l=LW)
                flat = leaf_mask[u][:].rearrange("p l k a -> p (l k a)")
                for l in range(4):
                    w = 8 >> l
                    mk = flat[:, l * n * 8:(l + 1) * n * 8].rearrange("p (a k) -> p a k", a=4).unsqueeze(3)
                    last = v.copy_predicated(view[:, :, :, 0:w], mk.to_broadcast([P, 4, per * 8, w]), view[:, :, :, w:2 * w])
                    if l < 3:
                        dve.drain()
                last.then_inc(picked, 1)

            use8, ahead, t0, t1_, slot_l, pos, dif, _ = sm

            def count_rows():
                dve.wait_ge(norm_ok, NGH)
                dve.wait_ge(consts, 4)
                ts(use8[:], norm2[:], THR, None, ALU.is_gt)
                v.memset(ahead[:, 0:1], 0.0)
                dve.drain()
                v.tensor_copy(ahead[:, 1:], use8[:, :NGH - 1])
                dve.drain()
                cur, other = ahead, t0
                for s in (1, 2, 4, 8):
                    v.tensor_copy(other[:, 0:s], cur[:, 0:s])
                    tt(other[:, s:], cur[:, s:], cur[:, :NGH - s], ALU.add)
                    dve.drain()
                    cur, other = other, cur
                assert cur is ahead
                tt(sc[0][:], ahead[:, NGH - 1:], use8[:, NGH - 1:], ALU.add).then_inc(rank, 1)
            def place_rows():
                dve.wait_ge(rank_mm, 1)
                v.tensor_copy(pos[:], ps[:, 5, 0:NGH])
                ts(si[0][:], ps[:, 5, 32:33], float(P - 1), None, ALU.add).then_inc(rank, 1)
                dve.drain()
                ts(si[1][:], si[0][:], 7, 7, ALU.logical_shift_right, ALU.logical_shift_left)
                dve.drain()
                v.tensor_copy(sc[1][:], si[1][:])
                tt(slot_l[:], elem_f[:], pos[:], ALU.subtract)
                dve.drain()
                ts(slot_l[:], slot_l[:], sc[1][:], None, ALU.add)
                dve.drain()
                tt(dif[:], pos[:], slot_l[:], ALU.subtract)
                dve.drain()
                tt(dif[:], dif[:], use8[:], ALU.mult)
                dve.drain()
                tt(slots[:], dif[:], slot_l[:], ALU.add).then_inc(rank, 1)
                ts(table_off[:], tile_at[:], sc[1][0:1, :], float(KT * O), ALU.is_ge, ALU.mult)

            def chunk(c, n, n_next):
                for t in range(KT):
                    pick(c, t, n)
                    if is_int(c) and c == 0 and t == 0:
                        place_rows()
                    if t % 4 == 3 and n_next:
                        one_hot(c + 1, t // 4, n_next)

            dve.drain()
            dve.wait_ge(conv_mm, C)
            one_hot(0, 0, CG)
            one_hot(0, 1, CG)
            count_rows()
            chunk(0, CG, CG)
            with dve.Fori(1, NCH - 1) as c:
                chunk(c, CG, CG)
            dve.wait_ge(ids_ld, 16)
            ts(gather_id[:], ids_sb[:], float(ROWS - 1), None, ALU.min).then_inc(rank, 1)
            chunk(NCH - 1, CG, LAST)
            chunk(NCH, LAST, 0)

            def x_low(k, u):
                dve.wait_ge(x_hi_ok, k + 1)
                wait_pos(dve, main1, k - 1)
                tt(x_lo[u][:], banks(0), x_hi[u][:].bitcast(F32), ALU.subtract).then_inc(x_lo_ok, 1)

            def result(k, u):
                dve.wait_ge(main1, k + 1)
                dve.wait_ge(res_ok, k + 1)
                if not is_int(k) or k >= 2:
                    dve.wait_ge(st_out[u], 8 * (k - u))
                tt(yo[u][:], banks(2 + 2 * u), x1g[u][:], ALU.add).then_inc(yo_ok, 1)

            x_low(0, 0)
            for t in range(KT):
                dve.wait_ge(w_hi_ok, t + 1)
                tt(w_lo[:, :, t, :], w1[:, :, t, :], w_hi[:, :, t, :].bitcast(F32), ALU.subtract).then_inc(w_lo_ok, 1)
            x_low(1, 1)
            result(0, 0)
            x_low(2, 0)
            result(1, 1)
            with dve.Fori(1, NR // 2) as i:
                x_low(2 * i + 1, 1)
                result(2 * i, 0)
                x_low(2 * i + 2, 0)
                result(2 * i + 1, 1)
            result(TILES - 1, 0)


_INS = ['x', 'itok_B_0_15', 'itok_B_8_3872', 'L0_cond_weights', 'L0_ffn_qweight', 'L0_ffn_weight_scale',
        'L0_ffn_weight_zero_point', 'L0_ffn_bias', 'L1_cond_log_dt', 'L1_cond_C', 'L1_cond_log_A_real',
        'L1_cond_A_imag', 'L1_cond_D', 'L1_ffn_qweight', 'L1_ffn_lut4', 'L1_ffn_lut8', 'L1_ffn_bias']
_OUTS = [((32, 64, 1024), 'float32')]


def kernel(**inputs):
    import numpy as _np
    import concourse.bacc as _bacc
    from concourse import mybir as _mybir
    from concourse.bass_utils import run_bass_kernel_spmd as _run

    nc = _bacc.Bacc("TRN2", target_bir_lowering=False, num_devices=1)
    arrays, args = {}, []
    for name in _INS:
        a = _np.ascontiguousarray(inputs[name])
        arrays[f"in_{name}_dram"] = a
        args.append(nc.dram_tensor(f"in_{name}_dram", a.shape, _mybir.dt.from_np(a.dtype), kind="ExternalInput").ap())
    for i, (shape, dtype) in enumerate(_OUTS):
        dt = _mybir.dt.from_np(_np.dtype(dtype))
        args.append(nc.dram_tensor(f"out_{i}_dram", shape, dt, kind="ExternalOutput").ap())
    adaln_ffn_kernel(nc, *args)
    r = _run(nc, [arrays], core_ids=[0])
    return r.results[0]["out_0_dram"]
```

```python
import math

import concourse.bass as bass
from concourse import mybir


def adaln_ffn_kernel(nc, x, cond_id, length, cond_w, q0, scale0, zero0, bias0,
                     log_dt, cmat, log_a_real, a_imag, dvec, q1, lut4, lut8, bias1, out):
    F32, F32R, BF16 = mybir.dt.float32, mybir.dt.float32r, mybir.dt.bfloat16
    I32, U16, U8 = mybir.dt.int32, mybir.dt.uint16, mybir.dt.uint8
    ALU, ACT = mybir.AluOpType, mybir.ActivationFunctionType
    ds = bass.ds

    B, C, T = x.shape
    NST = a_imag.shape[1]
    P = 128
    ROWS = B * C
    NR = ROWS // P
    KT = T // P
    GRP = q0.shape[1] // 3
    O = T
    NG = O // 8
    BLK = T // P
    GH = 4
    NGH = C // GH
    assert 2 * GH <= C // (NR // 2)
    CG, NCH = 12, 10
    LAST = NG - CG * NCH
    LW = 17
    TILES = NR + 1
    PAD_ID = 2 * ROWS
    KH = C // (NR // 2)
    LG = NG // (NR // 2)
    THR = float(2.0 ** 12 + 2.0 ** -11)
    MAGIC = 1.5 * 2.0 ** 23
    TAU = 2.0 * math.pi

    kpad = nc.dram_tensor("kpad", [C, P + T], F32).ap()
    x1_dram = nc.dram_tensor("x1_dram", [ROWS, T], F32).ap()
    xc_dram = nc.dram_tensor("xc_dram", [ROWS, T], F32).ap()
    ids_dram = nc.dram_tensor("ids_dram", [TILES * P, 1], I32).ap()

    used = [(nc.sbuf_base + 31) // 32 * 32]

    def region(nbytes):
        at = used[0]
        used[0] += nbytes
        return at

    def at(name, shape, dt, offset):
        return nc.alloc_sbuf_tensor_at(name, shape, dt, offset=offset)

    r_const = region(6 * 1024)
    r_main = region(64 * 1024)
    r_weights = region(32 * 1024)
    r_work = region(43 * 1024)
    r_table = region(60 * 1024)
    assert used[0] <= nc.sbuf_usable_end, (used[0], nc.sbuf_usable_end)

    def packer(start, size):
        pos = [start]

        def put(name, shape, dt):
            n = 1
            for s in shape[1:]:
                n *= s
            n *= {F32: 4, F32R: 4, I32: 4, BF16: 2, U16: 2, U8: 1}[dt]
            n = (n + 31) // 32 * 32
            t = at(name, shape, dt, pos[0])
            pos[0] += n
            assert pos[0] <= start + size, name
            return t
        return put

    const = packer(r_const, 6 * 1024)
    ident = const("ident", [P, P], F32)
    ident_bf = const("ident_bf", [P, P], BF16)
    half_id = const("half_id", [P, P], BF16)
    before = const("before", [P, P], F32)
    ones = const("ones", [P, P], F32)
    mask_t = const("mask_t", [P, BLK, B], F32)
    own_block = const("own_block", [P, 8], BF16)
    chan = const("chan", [P, 1], I32)
    code_mask = const("code_mask", [P, 4], I32)
    len_bc = const("len_bc", [P, B], I32)
    len_p = const("len_p", [P, 1], I32)
    len_pf = const("len_pf", [P, 1], F32)
    last_row = const("last_row", [1, 32], F32)
    gate = const("gate", [1, 1], F32)
    cond_sb = const("cond_sb", [1, B], I32)
    shift = const("shift", [P, 1], F32)
    xsum = const("xsum", [P, 2], F32)
    s_sb = const("s_sb", [P, 2], F32)
    norm_new = const("norm_new", [P, 2], F32)
    norm2 = const("norm2", [P, NGH], F32)
    d_sb = const("d_sb", [1, C], F32)
    d_now = const("d_now", [1, KH], F32)
    ids_sb = const("ids_sb", [P, TILES], I32)
    gather_id = const("gather_id", [P, TILES], I32)
    table_off = const("table_off", [1, TILES], I32)

    codes_i = at("codes_i", [P, 8, 4, GRP], I32, r_main)
    codes_b = at("codes_b", [P, 8, 4 * GRP], BF16, r_main + 32 * 1024)
    x1t = at("x1t", [P, C, BLK, B], F32, r_main)
    w1 = at("w1", [P, 2, KT, O], F32, r_main)
    w_lo = at("w_lo", [P, 2, KT, O], F32R, r_main)
    w_hi = at("w_hi", [P, 2, KT, O], F32R, r_table - 4 * 1024)

    q_t = at("q_t", [P, KT, O], F32R, r_weights)
    toep = at("toep", [P, 8, T], F32, r_weights)
    onehot = [at(f"onehot{h}", [P, CG, 8, 64], BF16, r_weights + h * 12288) for h in range(2)]
    ffn = packer(r_weights, 32 * 1024)
    x_hi = [ffn(f"x_hi{u}", [P, T], F32R) for u in range(2)]
    x_lo = [ffn(f"x_lo{u}", [P, T], F32R) for u in range(2)]
    yo = [ffn(f"yo{u}", [P, T], F32) for u in range(2)]
    xg = [ffn(f"xg{u}", [P, T], F32) for u in range(2)]

    LUT_F = LW * NG * 4
    raw0 = at("raw0", [P, 8, 3 * GRP], I32, r_work)
    lut_rest = at("lut_rest", [P, LW, NG], F32, r_work)
    lut_nat = at("lut_nat", [P, 8, 256], F32, r_work)
    lut4_nat = at("lut4_nat", [P, 8, 16], F32, r_work + 8192)
    lut_cols = at("lut_cols", [P, LW, P], F32, r_work + LUT_F)
    lutc = at("lutc", [P, 3, NG, LW], BF16, r_work + 2 * LUT_F)
    work = packer(r_work + LUT_F, LUT_F)
    waves = work("waves", [P, 3, KH, 32], F32)
    damps = work("damps", [P, 3, KH, 32], F32)
    e_long = work("e_long", [P, KH, 32], F32)
    e_short = work("e_short", [P, KH, 32], F32)
    after_lutc = r_work + 2 * LUT_F + 3 * NG * LW * 2
    work = packer(after_lutc, r_table - after_lutc)
    nat = [work(f"nat{n}", [C, NST], F32) for n in range(24)]
    nat2 = [work(f"nat2_{n}", [C, 2 * NST], F32) for n in range(4)]
    par = [work(f"par{n}", [P, C], F32) for n in range(4)]
    iota_m = work("iota_m", [P, 32], F32)
    zero_term = at("zero_term", [P, O], F32, after_lutc + 4096)
    natc = work("natc", [C, NST, 2], F32)
    logs, exps, expo, frac_ = [work(n, [C, NST + 1], F32) for n in ("logs", "exps", "expo", "frac_")]
    expo_i = work("expo_i", [C, NST + 1], I32)
    work = packer(r_work, 2 * LUT_F)
    yt = [work(f"yt{u}", [P, BLK, GH * B], F32) for u in range(2)]
    xr = [work(f"xr{u}", [P, T], F32) for u in range(2)]
    code8 = work("code8", [P, KT, NG], U8)
    bd0_at = after_lutc + 14 * 1024
    packed_at = bd0_at + 3 * CG * 8 * LW * 2
    work = packer(after_lutc, 14 * 1024)
    mask_row = work("mask_row", [P, T], F32)
    junk_c = work("junk_c", [P, T], BF16)
    bits = work("bits", [P, 4, KT * P], BF16)
    work = packer(bd0_at, packed_at - bd0_at)
    plane_words = work("plane_words", [P, 4, 32], I32)
    rep_words = work("rep_words", [P, 4, 16 * 32], I32)
    work = packer(r_work, 2 * LUT_F)
    bd1 = work("bd1", [P, 3, CG, 8 * LW], BF16)
    x1g = [work("x1g0", [P, T], F32)]
    work = packer(after_lutc, 14 * 1024)
    x1g.append(work("x1g1", [P, T], F32))
    bias1_bc = work("bias1_bc", [P, O], F32)
    leaf_mask = [work(f"leaf_mask{u}", [P, 4, CG, 8], U8) for u in range(2)]
    sm = [work(f"sm{n}", [P, NGH], F32) for n in range(8)]
    sc = [work(f"sc{n}", [P, 1], F32) for n in range(3)]
    si = [work(f"si{n}", [P, 1], I32) for n in range(2)]
    slots = work("slots", [P, NGH], I32)
    rowid = work("rowid", [P, NGH], I32)
    elem_f = work("elem_f", [P, NGH], F32)
    tile_at = work("tile_at", [1, TILES], F32)
    pad_ids = work("pad_ids", [TILES, P], I32)
    bd = [at("bd0", [P, 3, CG, 8 * LW], BF16, bd0_at), bd1]

    tiles = packer(r_table, 60 * 1024)
    scale_bc = tiles("scale_bc", [P, O], F32)
    nzs_bc = tiles("nzs_bc", [P, O], F32)
    bias0_bc = tiles("bias0_bc", [P, O], F32)
    ht = [[tiles(f"ht{u}{p}", [P, KT, P], F32R) for p in range(2)] for u in range(2)]
    xt = [tiles(f"xt{u}", [P, T], F32) for u in range(2)]
    xb = [tiles(f"xb{u}", [P, T], F32) for u in range(2)]
    x1 = [tiles(f"x1_{u}", [P, T], F32) for u in range(2)]
    prod = tiles("prod", [P, T], F32)
    wbd = tiles("wbd", [P, 2, P], F32)
    junk = tiles("junk", [P, T], BF16)
    kernels = tiles("kernels", [32, KH, 32], F32)
    tab = packer(packed_at, r_table + 60 * 1024 - packed_at)
    packed = tab("packed", [P, NG * 32], I32)
    MC = KT * 4 * CG * 8
    sel = tab("sel", [P, (NCH + 1) * MC], U8)

    ps = nc.alloc_psum_tensor("ps", [P, 8, 512], F32)

    def banks(a, n=2):
        return ps[:, a:a + n, :].rearrange("p a n -> p (a n)")

    SORT_AT = 448
    assert CG // 4 * 8 * LW <= SORT_AT
    ranks, total8 = ps[:, 5, SORT_AT:SORT_AT + NGH], ps[:, 5, SORT_AT + 32:SORT_AT + 33]

    def sem(name):
        return nc.alloc_semaphore(name)

    consts = sem("consts")
    ld_ssm = sem("ld_ssm")
    ld_small = sem("ld_small")
    ld_q0 = [sem(f"ld_q0{n}") for n in range(4)]
    ld_bc = sem("ld_bc")
    angles_ok = sem("angles_ok")
    exps_ok = sem("exps_ok")
    param_ok = sem("param_ok")
    par_ok = sem("par_ok")
    code_un = sem("code_un")
    code_cv = sem("code_cv")
    qt_mm = sem("qt_mm")
    qt_ev = [sem(f"qt_ev{u}") for u in range(2)]
    phase_ok = sem("phase_ok")
    wave_ok = sem("wave_ok")
    e_ok = sem("e_ok")
    k_mm = sem("k_mm")
    k_ev = sem("k_ev")
    kp_dma = sem("kp_dma")
    ld_x = [sem(f"ld_x{u}") for u in range(2)]
    ld_w = [sem(f"ld_w{u}") for u in range(2)]
    xsum_ok = sem("xsum_ok")
    x_read = sem("x_read")
    xb_ok = sem("xb_ok")
    zero_ok = sem("zero_ok")
    nzs_ok = sem("nzs_ok")
    h_mm = sem("h_mm")
    h_hi = sem("h_hi")
    h_lo = sem("h_lo")
    main0 = sem("main0")
    x1_ok = sem("x1_ok")
    x1_tr = sem("x1_tr")
    x1t_ok = sem("x1t_ok")
    st_x1 = [sem(f"st_x1{u}") for u in range(2)]
    ld_t = [sem(f"ld_t{n}") for n in range(2 * GH)]
    conv_mm = sem("conv_mm")
    yt_ok = sem("yt_ok")
    row_tr = sem("row_tr")
    xr_ok = sem("xr_ok")
    norm_ok = sem("norm_ok")
    st_xc = [sem(f"st_xc{u}") for u in range(2)]
    ld_words = sem("ld_words")
    ld_rep = sem("ld_rep")
    words_read = sem("words_read")
    bits_ok = sem("bits_ok")
    pack_ok = sem("pack_ok")
    code_mm = sem("code_mm")
    code_ok = sem("code_ok")
    sel_ok = sem("sel_ok")
    ld_lut = sem("ld_lut")
    lut_mm = sem("lut_mm")
    lut_hi = sem("lut_hi")
    lut_ok = sem("lut_ok")
    rank = sem("rank")
    ids_pad = sem("ids_pad")
    ids_sc = sem("ids_sc")
    ids_ld = sem("ids_ld")
    bd_ok = sem("bd_ok")
    oh_ok = sem("oh_ok")
    leaves = sem("leaves")
    mask_cp = sem("mask_cp")
    picked = sem("picked")
    w_ok = sem("w_ok")
    ld_b1 = sem("ld_b1")
    gat = [sem(f"gat{u}") for u in range(2)]
    gat1 = [sem(f"gat1{u}") for u in range(2)]
    w4_hi_ok = sem("w4_hi_ok")
    w4_lo_ok = sem("w4_lo_ok")
    w8_hi_ok = sem("w8_hi_ok")
    w8_lo_ok = sem("w8_lo_ok")
    xc_tr = sem("xc_tr")
    x_hi_ok = sem("x_hi_ok")
    x_lo_ok = sem("x_lo_ok")
    res_ok = sem("res_ok")
    main1 = sem("main1")
    yo_ok = sem("yo_ok")
    st_out = [sem(f"st_out{u}") for u in range(2)]

    LUT_ROUNDS = ((0, 8), (8, 8), (16, LW - 16))

    def pairs(eng, n, step):
        step(0, 0, 0)
        step(1, 1, 0)
        with eng.Fori(1, n // 2 - 1) as i:
            step(2 * i, 0, i)
            step(2 * i + 1, 1, i)
        step(n - 2, 0, n // 2 - 1)
        step(n - 1, 1, n // 2 - 1)

    def is_int(v):
        return isinstance(v, int)

    def wait_pos(eng, s, v):
        if not is_int(v) or v > 0:
            eng.wait_ge(s, v)

    def group_rows(dram, g, hh):
        return dram.rearrange("(b c) t -> c b t", c=C)[ds(GH * g + hh, 1), :, :].rearrange("a b t -> (a b) t")

    block = nc.Block()
    with block:

        @block.sync
        def _(sp):
            sp.dma_start(logs[:, NST:], log_dt.rearrange("(c a) -> c a", a=1)).then_inc(ld_ssm, 16)
            sp.dma_start(logs[:, 0:NST], log_a_real).then_inc(ld_ssm, 16)
            sp.dma_start(nat[1][:], a_imag).then_inc(ld_ssm, 16)
            for n in range(4):
                sp.dma_start(raw0[:, 2 * n:2 * n + 2, :],
                             q0[2 * n * P:(2 * n + 2) * P, :].rearrange("(t p) k -> p t k", p=P)).then_inc(ld_q0[n], 16)
            sp.dma_start(natc[:], cmat).then_inc(ld_small, 16)
            sp.dma_start(d_sb[:], dvec.rearrange("(a c) -> a c", a=1)).then_inc(ld_small, 16)
            sp.dma_start(cond_sb[:], cond_id.rearrange("(a c) -> a c", a=1)).then_inc(ld_small, 16)
            sp.dma_start(len_bc[:], bass.AP(tensor=length.tensor, offset=0, ap=[[0, P], [1, B]])).then_inc(ld_small, 16)
            for q in range(GH):
                sp.dma_start(len_p[q * B:(q + 1) * B, :], length.rearrange("(b a) -> b a", a=1)).then_inc(ld_small, 16)
            sp.dma_start(scale_bc[:], bass.AP(tensor=scale0.tensor, offset=0, ap=[[0, P], [1, O]])).then_inc(ld_bc, 16)
            sp.dma_start(nzs_bc[:], bass.AP(tensor=zero0.tensor, offset=0, ap=[[0, P], [1, O]])).then_inc(ld_bc, 16)
            sp.dma_start(bias0_bc[:], bass.AP(tensor=bias0.tensor, offset=0, ap=[[0, P], [1, O]])).then_inc(ld_bc, 16)


            def load_x(r, u):
                sp.dma_start(xt[u][:], x.rearrange("b c t -> (b c) t")[ds(r * P, P), :]).then_inc(ld_x[u], 16)
                for b2 in range(2):
                    which = sp.value_load(cond_sb[0:1, ds(2 * r + b2, 1)], min_val=0, max_val=cond_w.shape[0] - 1)
                    sp.dma_start(wbd[b2 * C:(b2 + 1) * C, u, b2 * C:(b2 + 1) * C],
                                 cond_w[ds(which, 1), :, :].rearrange("a c d -> (a c) d")).then_inc(ld_w[u], 16)

            sp.wait_ge(ld_small, 16 * (4 + GH))
            sp.wait_ge(consts, 1)
            load_x(0, 0)
            load_x(1, 1)

            sp.wait_ge(consts, 2)
            sp.dma_start(kpad[:, T:], prod[0:C, 0:P]).then_inc(kp_dma, 16)
            sp.wait_ge(code_un, 4)
            sp.dma_start(lut_nat[:], lut8.rearrange("(a g) c -> g a c", a=8)).then_inc(ld_lut, 16)
            sp.dma_start(lut4_nat[:], lut4.rearrange("(a g) c -> g a c", a=8)).then_inc(ld_lut, 16)

            def store_kernels(j):
                sp.wait_ge(k_ev, j + 1)
                dst = kpad[ds(KH * j, KH), 0:T].rearrange("h (p m) -> p h m", m=32)
                sp.dma_start(dst, kernels[:]).then_inc(kp_dma, 16)

            def load_toep(g, u):
                for hh in range(GH):
                    if not is_int(g) or g >= 2:
                        sp.wait_ge(conv_mm, GH * (g - 2) + hh + 1)
                    src = kpad[ds(GH * g + hh, 1), :]
                    src = bass.AP(tensor=src.tensor, offset=src.offset, ap=[[1, P], [1, T]])
                    sp.dma_start(toep[:, GH * u + hh, :], src).then_inc(ld_t[GH * u + hh], 16)

            def layer0(r, u, i):
                if not is_int(r) or r < NR - 2:
                    sp.wait_ge(h_mm, r + 1)
                    sp.wait_ge(x_read, r + 1)
                    load_x(r + 2, u)
                if is_int(r) and r == NR - 1:
                    sp.wait_ge(main0, NR)
                    sp.wait_ge(kp_dma, 32)
                    load_toep(0, 0)
                    load_toep(1, 1)
                sp.wait_ge(x1_ok, r + 1)
                sp.dma_start(x1_dram[ds(r * P, P), :], x1[u][:]).then_inc(st_x1[u], 16)
                if u == 1 and not (is_int(i) and i == 0):
                    store_kernels(i - 1)

            pairs(sp, NR, layer0)

            store_kernels(NR // 2 - 1)
            sp.wait_ge(kp_dma, 16 * (NR // 2 + 1))
            with sp.Fori(1, NGH // 2) as i:
                load_toep(2 * i, 0)
                load_toep(2 * i + 1, 1)

            sp.wait_ge(norm_ok, NGH)
            sp.wait_ge(code_mm, 8)
            sp.dma_start(bias1_bc[:], bass.AP(tensor=bias1.tensor, offset=0, ap=[[0, P], [1, O]])).then_inc(ld_b1, 16)

        @block.gpsimd
        def _(pool):
            g = nc.gpsimd

            def eye(t, base, mult, cmp, fill, src=None):
                g.affine_select(out=t, in_=t, compare_op=cmp, fill=fill, base=base, pattern=[[mult, P]],
                                channel_multiplier=1)

            g.memset(wbd[:], 0.0).then_inc(consts, 1)
            g.memset(shift[:], 0.25)
            g.memset(last_row[:], 0.0)
            pool.drain()
            g.memset(last_row[:, 31:32], 1.0)
            g.memset(shift[NST:, :], 0.0)
            pool.drain()
            g.memset(ident[:], 0.0)
            g.memset(ident_bf[:], 0.0)
            g.memset(half_id[:], 0.0)
            g.memset(ones[:], 1.0)
            g.memset(before[:], 1.0)
            g.memset(own_block[:], 1.0)
            pool.drain()
            eye(ident[:], 0, -1, ALU.not_equal, 1.0)
            eye(ident_bf[:], 0, -1, ALU.not_equal, 1.0)
            eye(half_id[:], 0, -1, ALU.not_equal, 0.5)
            g.affine_select(out=before[:], in_=before[:], compare_op=ALU.is_ge, fill=0.0, base=-1,
                            pattern=[[1, P]], channel_multiplier=-1)
            g.affine_select(out=own_block[:], in_=own_block[:], compare_op=ALU.is_ge, fill=0.0, base=0,
                            pattern=[[-16, 8]], channel_multiplier=1)
            pool.drain()
            g.affine_select(out=own_block[:], in_=own_block[:], compare_op=ALU.is_ge, fill=0.0, base=15,
                            pattern=[[16, 8]], channel_multiplier=-1)
            g.iota(chan[:], pattern=[[0, 1]], base=0, channel_multiplier=1)
            g.iota(iota_m[:], pattern=[[1, 32]], base=0, channel_multiplier=0, allow_small_or_imprecise_dtypes=True)
            g.iota(mask_t[:].bitcast(I32), pattern=[[P, BLK], [0, B]], base=0, channel_multiplier=1)
            pool.drain()
            g.memset(prod[0:C, 0:P], 0.0).then_inc(consts, 1)
            pool.wait_ge(ld_bc, 48)

            def split_table(j):
                rest = lut_rest[:, :, ds(LG * j, LG)].rearrange("p l g -> p g l")
                for part in (1, 2):
                    pool.drain()
                    g.tensor_tensor(rest, rest, lutc[:, part - 1, ds(LG * j, LG), :], ALU.subtract)
                    pool.drain()
                    last = g.tensor_copy(lutc[:, part, ds(LG * j, LG), :], rest)
                last.then_inc(lut_ok, 1)

            def layer0(r, u, i):
                pool.wait_ge(ld_x[u], 8 * (r + 2 - u))
                wait_pos(pool, x1_ok, r - 1)
                g.tensor_tensor(xb[u][:], xt[u][:], bias0_bc[:], ALU.add).then_inc(x_read, 1)
                pool.drain()
                pool.wait_ge(zero_ok, r + 1)
                g.tensor_tensor(xb[u][:], xb[u][:], zero_term[:], ALU.add).then_inc(xb_ok, 1)
                if u == 1:
                    if is_int(i) and i == 0:
                        pool.wait_ge(lut_hi, 5)
                    split_table(i)

            pairs(pool, NR, layer0)
            pool.wait_ge(param_ok, 1)
            g.iota(mask_row[:].bitcast(I32), pattern=[[1, T]], base=0, channel_multiplier=0).then_inc(consts, 1)

            def load_words(i):
                wait_pos(pool, words_read, i)
                wait_pos(pool, pack_ok, i)
                pool.dma_start(plane_words[:], q1[4:8, ds(i * P, P), :].rearrange("k g w -> g k w")).then_inc(ld_words, 16)
                for a in range(8):
                    src = q1[0:4, ds(a * P + i * 16, 16), :]
                    src = bass.AP(tensor=src.tensor, offset=src.offset, ap=[[0, 16], [O * 32, 4], [1, 16 * 32]])
                    pool.dma_start(rep_words[16 * a:16 * a + 16, :, :], src).then_inc(ld_rep, 16)

            pool.drain()
            pool.wait_ge(x1_ok, NR)
            for n in range(GH):
                pool.wait_ge(ld_t[n], 16)
            load_words(0)
            with pool.Fori(1, 8) as i:
                load_words(i)

            def block_diag(c, u, n):
                if not is_int(c) or c >= 2:
                    pool.wait_ge(leaves, KT * (c - 1))
                for part in range(3):
                    last = g.tensor_tensor(
                        bd[u][:, part, 0:n, :].rearrange("p k (a l) -> p k a l", a=8),
                        lutc[:, part, ds(CG * c, n), :].unsqueeze(2).to_broadcast([P, n, 8, LW]),
                        own_block[:].unsqueeze(1).unsqueeze(3).to_broadcast([P, n, 8, LW]), ALU.mult)
                last.then_inc(bd_ok, 1)

            pool.wait_ge(words_read, 8)
            pool.wait_ge(pack_ok, 8)
            block_diag(0, 0, CG)
            pool.wait_ge(code_mm, 8)

            for q in range(GH):
                g.iota(rowid[q * B:(q + 1) * B, :], pattern=[[GH, NGH]], base=q, channel_multiplier=C)
                pool.drain()
            g.iota(elem_f[:], pattern=[[P, NGH]], base=0, channel_multiplier=1, allow_small_or_imprecise_dtypes=True)
            g.iota(tile_at[:], pattern=[[P, TILES]], base=0, channel_multiplier=0, allow_small_or_imprecise_dtypes=True)
            pool.drain()
            g.memset(pad_ids[:], PAD_ID).then_inc(consts, 1)
            pool.wait_ge(consts, 4)
            pool.dma_start(ids_dram.rearrange("(t p) a -> t (p a)", p=P), pad_ids[:]).then_inc(ids_pad, 16)
            pool.wait_ge(ids_pad, 16)
            pool.wait_ge(norm_ok, NGH)
            for u in range(2):
                pool.wait_ge(st_xc[u], 16 * GH * NGH // 2)
            block_diag(1, 1, CG)
            pool.wait_ge(rank, 3)
            for k in range(NGH):
                pool.indirect_dma_start(ids_dram[:, :], bass.IndirectOffsetOnAxis(ap=slots[:, k:k + 1], axis=0),
                                        rowid[:, k:k + 1], None,
                                        bounds_check=TILES * P - 1, oob_is_err=False).then_inc(ids_sc, 16)

            pool.wait_ge(ids_sc, 16 * NGH)
            pool.dma_start(ids_sb[:], ids_dram.rearrange("(t p) a -> p (t a)", p=P),
                           allow_slow_non_contiguous=True).then_inc(ids_ld, 16)
            with pool.Fori(1, NCH // 2) as i:
                block_diag(2 * i, 0, CG)
                block_diag(2 * i + 1, 1, CG)
            block_diag(NCH, 0, LAST)

            pool.wait_ge(rank, 4)
            pool.wait_ge(ld_b1, 16)

            def gather_xc(k, u):
                pool.indirect_dma_start(xg[u][:], None, xc_dram[:, :],
                                        bass.IndirectOffsetOnAxis(ap=gather_id[:, k:k + 1], axis=0),
                                        bounds_check=ROWS - 1, oob_is_err=False).then_inc(gat[u], 16)

            def gather_x1(k, u):
                pool.indirect_dma_start(x1g[u][:], None, x1_dram[:, :],
                                        bass.IndirectOffsetOnAxis(ap=gather_id[:, k:k + 1], axis=0),
                                        bounds_check=ROWS - 1, oob_is_err=False).then_inc(gat1[u], 16)

            for u in range(2):
                pool.wait_ge(st_x1[u], 16 * NR // 2)
            for k in range(2):
                gather_xc(k, k)
                gather_x1(k, k)
            for t in range(KT - 1):
                pool.wait_ge(w4_hi_ok, t + 1)
                g.tensor_tensor(w_lo[:, 1, t, :], w1[:, 1, t, :], w_hi[:, 1, t, :].bitcast(F32),
                                ALU.subtract).then_inc(w4_lo_ok, 1)
            for k in range(TILES):
                u = k % 2
                if k + 2 < TILES:
                    pool.wait_ge(xc_tr, k + 1)
                    gather_xc(k + 2, u)
                pool.wait_ge(gat1[u], 16 * (k // 2 + 1))
                g.tensor_tensor(x1g[u][:], x1g[u][:], bias1_bc[:], ALU.add).then_inc(res_ok, 1)
                pool.wait_ge(yo_ok, k + 1)
                pool.indirect_dma_start(out.rearrange("b c t -> (b c) t"),
                                        bass.IndirectOffsetOnAxis(ap=ids_sb[:, k:k + 1], axis=0),
                                        yo[u][:], None, bounds_check=ROWS - 1, oob_is_err=False).then_inc(st_out[u], 16)
                if k + 2 < TILES:
                    gather_x1(k + 2, u)
            pool.wait_ge(st_out[0], 16 * ((TILES + 1) // 2))
            pool.wait_ge(st_out[1], 16 * (TILES // 2))

        @block.scalar
        def _(act):
            a = nc.scalar
            (lar, aim, ear, adt, wdt, th, ea, em1, fr, fr2, sn, sh, cm1, cs1, zr, zi, nr_, ni_, m2, tmp,
             tmp2, tmp3, csr, csi) = nat
            act.wait_ge(angles_ok, 1)
            a.activation(ea[:], adt[:], ACT.Exp)
            a.activation(th[:], adt[:], ACT.Tanh, scale=0.5)
            a.activation(sn[:], fr[:], ACT.Sin, scale=TAU)
            a.activation(sh[:], fr2[:], ACT.Sin, scale=TAU).then_inc(exps_ok, 1)

            for n in range(4):
                act.wait_ge(code_un, n + 1)
                a.activation(codes_b[:, 2 * n:2 * n + 2, :].rearrange("p t k -> p (t k)"),
                             codes_i[:, 2 * n:2 * n + 2].rearrange("p t v k -> p (t v k)"),
                             ACT.Copy, bias=-32.0).then_inc(code_cv, 2)
            def x_sum(r, u):
                act.drain()
                act.wait_ge(ld_x[u], 8 * (r + 2 - u))
                wait_pos(act, h_mm, r - 1)
                a.activation(junk[:], xt[u][:], ACT.Copy, accum_out=xsum[:, u:u + 1]).then_inc(xsum_ok, 1)

            x_sum(0, 0)
            for n in range(4):
                act.wait_ge(qt_mm, 2 * n + 1)
                a.activation(q_t[:, :, 2 * n * P:(2 * n + 1) * P],
                             banks(2).rearrange("p (k n) -> p k n", n=P), ACT.Copy).then_inc(qt_ev[0], 2)

            def high_part(r, u):
                act.wait_ge(h_mm, r + 1)
                wait_pos(act, main0, r - 1)
                a.activation(ht[u][0][:].rearrange("p k r -> p (k r)"), banks(0), ACT.Copy).then_inc(h_hi, 1)

            def zero_points(r, u):
                act.wait_ge(h_lo, r + 1)
                wait_pos(act, xb_ok, r)
                a.activation(zero_term[:], nzs_bc[:], ACT.Copy, scale=s_sb[:, u:u + 1]).then_inc(zero_ok, 1)

            x_sum(1, 1)
            high_part(0, 0)

            def table_columns():
                act.wait_ge(ld_lut, 32)
                a.activation(lut_cols[:, 0:16, :].rearrange("p h (a l) -> p h a l", l=16),
                             lut_nat[:].rearrange("p a (h l) -> p h a l", l=16), ACT.Copy)
                a.activation(lut_cols[:, 16, :], lut4_nat[:].rearrange("p a l -> p (a l)"), ACT.Copy).then_inc(lut_hi, 1)

            def table_half(n):
                first, count = LUT_ROUNDS[n]
                act.wait_ge(lut_mm, n + 1)
                a.activation(lut_rest[:, first:first + count, :].rearrange("p l g -> p (l g)"),
                             banks(4)[:, 0:count * NG], ACT.Copy, scale=0.5).then_inc(lut_hi, 1)

            def kernel_waves(j):
                act.wait_ge(phase_ok, j + 1)
                a.activation(damps[:, 0], damps[:, 2], ACT.Exp, scale=32.0)
                a.activation(damps[:, 1], damps[:, 2], ACT.Exp)
                a.activation(waves[:], waves[:], ACT.Sin, scale=TAU).then_inc(wave_ok, 1)

            def copy_kernels(j, src):
                act.wait_ge(k_mm, j + 2)
                act.wait_ge(kp_dma, 16 * (j + 1))
                a.activation(kernels[:], src.rearrange("p (h m) -> p h m", m=32)[:, :, ::-1], ACT.Copy).then_inc(k_ev, 1)

            def layer0(r, u, i):
                if is_int(r) and r == 0:
                    high_part(1, 1)
                    table_columns()
                    table_half(0)
                    act.wait_ge(nzs_ok, 1)
                    act.wait_ge(k_mm, 1)
                    zero_points(0, 0)
                    table_half(1)
                    return
                zero_points(r, u)
                if not is_int(r) or r < NR - 1:
                    x_sum(r + 1, 1 - u)
                    high_part(r + 1, 1 - u)
                if is_int(r) and r == 1:
                    table_half(2)
                    act.drain()
                    a.activation(lutc[:, 0, :, :], lut_rest[:].rearrange("p l g -> p g l"), ACT.Copy).then_inc(lut_hi, 1)
                if not (is_int(i) and i == 0):
                    if u == 0:
                        kernel_waves(i - 1)
                    else:
                        copy_kernels(i - 1, ps[0:32, 7, 0:KH * 32])

            pairs(act, NR, layer0)
            kernel_waves(NR // 2 - 1)
            copy_kernels(NR // 2 - 1, ps[0:32, 2, 0:KH * 32])
            act.wait_ge(lut_ok, NR // 2)

            def norms(g, u):
                act.drain()
                act.wait_ge(xr_ok, g + 1)
                for hh in range(GH):
                    act.dma_start(group_rows(xc_dram, g, hh), xr[u][hh * B:(hh + 1) * B, :]).then_inc(st_xc[u], 16)
                a.activation(junk_c[:], xr[u][:], ACT.Square, accum_out=norm_new[:, u:u + 1])
                act.drain()
                a.activation(norm2[:, ds(g, 1)], norm_new[:, u:u + 1], ACT.Copy).then_inc(norm_ok, 1)

            def copy_out(g, u):
                act.wait_ge(conv_mm, GH * (g + 1))
                wait_pos(act, row_tr, g - 1)
                for hh in range(GH):
                    last = a.activation(yt[u][:, :, hh * B:(hh + 1) * B],
                                        banks(2 * u)[:, hh * BLK * B:(hh + 1) * BLK * B].rearrange("p (j b) -> p j b", b=B),
                                        ACT.Copy)
                last.then_inc(yt_ok, 1)
                if not is_int(g) or g > 0:
                    norms(g - 1, 1 - u)

            def codes(i):
                act.wait_ge(code_mm, i + 1)
                wait_pos(act, sel_ok, i)
                a.activation(code8[:].rearrange("p t g -> p (t g)"), banks(6), ACT.Copy).then_inc(code_ok, 1)

            copy_out(0, 0)
            copy_out(1, 1)
            codes(0)
            with act.Fori(1, 8) as i:
                copy_out(2 * i, 0)
                copy_out(2 * i + 1, 1)
                codes(i)
            norms(NGH - 1, 1)

            act.wait_ge(sel_ok, 8)

            def unit(c, uc, n):
                for t in range(KT):
                    u = t % 2
                    wait_pos(act, picked, KT * c + t - 1)
                    a.activation(leaf_mask[u][:].rearrange("p l k a -> p (l k a)")[:, 0:4 * n * 8],
                                 sel[:, ds(c * MC + t * 4 * n * 8, 4 * n * 8)], ACT.Copy).then_inc(mask_cp, 1)
                    if not (is_int(c) and c == 0 and t == 0):
                        store(c if t else c - 1, (t - 1) % KT, n if t else CG)
                    if is_int(c) and c == NCH and t:
                        high_weights(1, t - 1, w4_hi_ok)

            def high_weights(l, t, done):
                act.drain()
                a.activation(w_hi[:, l, t, :], w1[:, l, t, :], ACT.Copy).then_inc(done, 1)

            def store(c, t, n):
                u = t % 2
                act.wait_ge(picked, KT * c + t + 1)
                view = ps[:, 4 * u:4 * u + 4, 0:n // 4 * 8 * LW].rearrange("p a (k o l) -> p a k o l", o=8, l=LW)
                for l, leaf in ((0, 0), (1, 16)):
                    dst = w1[:, l, t, :].rearrange("p (o g) -> p g o", o=8)[:, ds(CG * c, n), :]
                    last = a.activation(dst.rearrange("p (a k) o -> p a k o", a=4), view[:, :, :, :, leaf], ACT.Copy)
                last.then_inc(w_ok, 1)

            unit(0, 0, CG)
            with act.Fori(1, NCH) as c:
                unit(c, 0, CG)
            unit(NCH, 0, LAST)

            def x_high(k, u):
                act.wait_ge(xc_tr, k + 1)
                wait_pos(act, main1, k - 1)
                a.activation(x_hi[u][:], banks(0), ACT.Copy).then_inc(x_hi_ok, 1)

            x_high(0, 0)
            store(NCH, KT - 1, LAST)
            for t in range(KT):
                high_weights(0, t, w8_hi_ok)
            high_weights(1, KT - 1, w4_hi_ok)
            x_high(1, 1)
            with act.Fori(1, NR // 2) as i:
                x_high(2 * i, 0)
                x_high(2 * i + 1, 1)
            x_high(TILES - 1, 0)

        @block.tensor
        def _(pe):
            mm = nc.tensor.matmul
            pe.wait_ge(consts, 2)

            def transpose_codes(n, u, i):
                pe.wait_ge(code_cv, n + 2 - u)
                wait_pos(pe, qt_ev[u], n - u)
                for k in range(KT):
                    last = mm(banks(2 + 2 * u)[:, k * P:(k + 1) * P],
                              codes_b[:, ds(n, 1), k * P:(k + 1) * P].rearrange("p a k -> p (a k)"),
                              ident_bf[:], start=True, stop=True)
                last.then_inc(qt_mm, 1)

            pairs(pe, 8, transpose_codes)
            def transpose_params():
                pe.wait_ge(param_ok, 1)
                for n in range(4):
                    last = nc.tensor.transpose(ps[:, 7, n * C:(n + 1) * C], nat2[n][:], ident[0:C, 0:C])
                last.then_inc(k_mm, 1)

            def transpose_table(n):
                first, count = LUT_ROUNDS[n]
                pe.wait_ge(lut_hi, n + 1)
                for hi in range(count):
                    last = nc.tensor.transpose(banks(4)[:, hi * P:(hi + 1) * P], lut_cols[:, first + hi, :], ident[:])
                last.then_inc(lut_mm, 1)

            def kernels_of(j, out):
                pe.wait_ge(e_ok, j + 1)
                for h in range(KH):
                    mm(out[:, h * 32:(h + 1) * 32], e_long[:, h, :], e_short[:, h, :], start=True, stop=False)
                    last = mm(out[:, h * 32:h * 32 + 1], last_row[:], d_now[:, h:h + 1], start=False, stop=True)
                last.then_inc(k_mm, 1)

            def mix(r, u):
                pe.wait_ge(ld_x[u], 8 * (r + 2 - u))
                pe.wait_ge(ld_w[u], 16 * (r + 2 - u))
                pe.wait_ge(xsum_ok, r + 1)
                for k in range(KT):
                    cols = xt[u][:].rearrange("p (g v) -> p v g", v=4)[:, k // 2, (k % 2) * P:(k % 2) * P + P]
                    mm(banks(0)[:, k * P:(k + 1) * P], cols, wbd[:, u, :], start=True, stop=True)
                mm(ps[:, 6, 0:1], wbd[:, u, :], xsum[:, u:u + 1], start=True, stop=True).then_inc(h_mm, 1)

            def layer0(r, u, i):
                pe.wait_ge(h_lo, r + 1)
                if not is_int(r) or r < NR - 1:
                    wait_pos(pe, x1t_ok, r - 1)
                    mix(r + 1, 1 - u)
                if u == 1 and not (is_int(i) and i == 0):
                    if is_int(i) and i == NR // 2 - 1:
                        pe.wait_ge(x1t_ok, r - 1)
                    kernels_of(i - 1, ps[0:32, 7, 0:KH * 32])
                if is_int(r) and r == 1:
                    transpose_table(2)
                    pe.wait_ge(lut_hi, 4)
                wait_pos(pe, x1_ok, r - 1)
                for half in range(2):
                    for k in range(KT):
                        for part in range(2):
                            last = mm(ps[:, 2 + 2 * u + half, :], ht[u][part][:, k, :],
                                      q_t[:, k, half * 512:(half + 1) * 512],
                                      start=(k == 0 and part == 0), stop=(k == KT - 1 and part == 1))
                    if half == 0 and (not is_int(r) or r > 0):
                        if not is_int(r) or r < NR - 1:
                            pe.wait_ge(h_lo, r + 2)
                        if is_int(r) and r == 1:
                            pe.wait_ge(par_ok, 1)
                        if u == 1 and not (is_int(i) and i == 0):
                            pe.wait_ge(k_ev, i)
                        transpose_x1(r - 1, 1 - u)
                    if is_int(r) and r == 0 and half == 0:
                        transpose_table(0)
                        transpose_params()
                last.then_inc(main0, 1)
                if is_int(r) and r == 0:
                    transpose_table(1)

            def transpose_x1(r, u):
                pe.wait_ge(x1_ok, r + 1)
                wait_pos(pe, x1t_ok, r)
                for k in range(BLK):
                    last = nc.tensor.transpose(banks(6)[:, k * P:(k + 1) * P], x1[u][:, k * P:(k + 1) * P], ident[:])
                last.then_inc(x1_tr, 1)

            mix(0, 0)
            pe.wait_ge(qt_ev[0], 8)
            pe.wait_ge(qt_ev[1], 8)
            pairs(pe, NR, layer0)
            transpose_x1(NR - 1, 1)

            pe.wait_ge(x1t_ok, NR)

            def conv(g, u):
                wait_pos(pe, yt_ok, g - 1)
                for hh in range(GH):
                    pe.wait_ge(ld_t[GH * u + hh], 8 * (g + 2 - u))
                    o0 = (hh % 2) * BLK * B
                    for d in range(BLK):
                        rhs = x1t[:, ds(GH * g + hh, 1), 0:BLK - d, :].rearrange("p a k b -> p (a k b)")
                        last = mm(ps[:, 2 * u + hh // 2, o0 + d * B:o0 + BLK * B],
                                  toep[:, GH * u + hh, (BLK - 1 - d) * P:(BLK - d) * P], rhs,
                                  start=(d == 0), stop=(d == BLK - 1))
                    last.then_inc(conv_mm, 1)

            def to_rows(g, u):
                pe.wait_ge(yt_ok, g + 1)
                wait_pos(pe, xr_ok, g)
                for k in range(BLK):
                    last = nc.tensor.transpose(banks(4)[:, k * P:(k + 1) * P], yt[u][:, k, :], ident[:])
                last.then_inc(row_tr, 1)

            def high_codes(i):
                pe.wait_ge(bits_ok, i + 1)
                wait_pos(pe, code_ok, i)
                for t in range(KT):
                    last = mm(banks(6)[:, t * NG:(t + 1) * NG], bits[:, 0, t * P:(t + 1) * P], half_id[:],
                              start=True, stop=True)
                last.then_inc(code_mm, 1)

            conv(0, 0)
            kernels_of(NR // 2 - 1, ps[0:32, 2, 0:KH * 32])
            pe.wait_ge(k_ev, NR // 2)
            conv(1, 1)
            to_rows(0, 0)
            high_codes(0)
            with pe.Fori(1, NGH // 2) as i:
                conv(2 * i, 0)
                to_rows(2 * i - 1, 1)
                conv(2 * i + 1, 1)
                to_rows(2 * i, 0)
                high_codes(i)
            to_rows(NGH - 1, 1)

            pe.wait_ge(yt_ok, NGH)

            def row_ranks():
                pe.wait_ge(rank, 1)
                mm(ranks, before[:], sm[0][:], start=True, stop=False)
                mm(ranks, ones[:], sm[1][:], start=False, stop=True)
                mm(total8, ones[:], sc[0][:], start=True, stop=True)

            def unit(c, uc, n):
                pe.wait_ge(bd_ok, c + 1)
                for t in range(KT):
                    u, half = t % 2, t // 4
                    pe.wait_ge(oh_ok, KT * c + t + 1)
                    wait_pos(pe, w_ok, KT * c + t - 1)
                    if is_int(c) and c == 0 and t == 3:
                        row_ranks()
                    for k in range(n):
                        lhs = onehot[half][:, k, 2 * (t % 4):2 * (t % 4) + 2, :].rearrange("p j w -> p (j w)")
                        per = n // 4
                        for part in range(3):
                            last = mm(ps[:, 4 * u + k // per, (k % per) * 8 * LW:(k % per + 1) * 8 * LW], lhs,
                                      bd[uc][:, part, k, :], start=(part == 0), stop=(part == 2))
                    last.then_inc(leaves, 1)
                    if is_int(c) and c == 0 and t == 0:
                        pe.wait_ge(xr_ok, NGH)
                        pe.wait_ge(code_ok, 8)

            unit(0, 0, CG)
            unit(1, 1, CG)
            with pe.Fori(1, NCH // 2) as i:
                unit(2 * i, 0, CG)
                unit(2 * i + 1, 1, CG)
            unit(NCH, 0, LAST)

            pe.wait_ge(w_ok, KT * (NCH + 1) - 1)
            pe.wait_ge(rank, 4)

            def to_cols(k, u):
                pe.wait_ge(gat[u], 8 * (k + 2 - u))
                wait_pos(pe, x_lo_ok, k)
                for t in range(KT):
                    last = nc.tensor.transpose(banks(0)[:, t * P:(t + 1) * P], xg[u][:, t * P:(t + 1) * P], ident[:])
                last.then_inc(xc_tr, 1)

            def ffn1(k, u):
                if not (is_int(k) and k == TILES - 1):
                    to_cols(k + 1, 1 - u)
                off = pe.value_load(table_off[0:1, ds(k, 1)], min_val=0, max_val=KT * O)
                pe.wait_ge(x_lo_ok, k + 1)
                wait_pos(pe, yo_ok, k - 1)
                hi = w_hi[:].rearrange("p l t o -> p (l t o)")
                lo = w_lo[:].rearrange("p l t o -> p (l t o)")
                for t in range(KT):
                    if is_int(k) and k == 0:
                        pe.wait_ge(w8_lo_ok, t + 1 if t < KT - 1 else KT + 1)
                        pe.wait_ge(w4_lo_ok, min(t + 1, KT - 1))
                    xh, xl = x_hi[u][:, t * P:(t + 1) * P], x_lo[u][:, t * P:(t + 1) * P]
                    for n, (xv, wv) in enumerate(((xh, hi), (xh, lo), (xl, hi))):
                        for half in range(2):
                            last = mm(ps[:, 2 + 2 * u + half, :], xv, wv[:, ds(off + t * O + half * 512, 512)],
                                      start=(t == 0 and n == 0), stop=(t == KT - 1 and n == 2))
                last.then_inc(main1, 1)

            to_cols(0, 0)
            ffn1(0, 0)
            ffn1(1, 1)
            with pe.Fori(1, NR // 2) as i:
                ffn1(2 * i, 0)
                ffn1(2 * i + 1, 1)
            ffn1(TILES - 1, 0)

        @block.vector
        def _(dve):
            v = nc.vector
            tt, ts, stt = v.tensor_tensor, v.tensor_scalar, v.scalar_tensor_tensor
            (lar, aim, ear, adt, wdt, th, ea, em1, fr, fr2, sn, sh, cm1, cs1, zr, zi, nr_, ni_, m2, tmp,
             tmp2, tmp3, csr, csi) = nat
            dve.wait_ge(ld_ssm, 48)
            ts(expo[:], logs[:], 1.0 / math.log(2.0), None, ALU.mult)
            dve.drain()
            ts(expo[:], expo[:], MAGIC, MAGIC, ALU.add, ALU.subtract)
            dve.drain()
            stt(frac_[:], expo[:], -0.693359375, logs[:], ALU.mult, ALU.add)
            ts(expo_i[:], expo[:], 127.0, None, ALU.add)
            dve.drain()
            stt(frac_[:], expo[:], 2.12194440e-4, frac_[:], ALU.mult, ALU.add)
            ts(expo_i[:], expo_i[:], 23, None, ALU.logical_shift_left)
            dve.drain()
            ts(exps[:], frac_[:], 1.0 / math.factorial(7), None, ALU.mult)
            for n in range(6, 0, -1):
                dve.drain()
                stt(exps[:], exps[:], 1.0 / math.factorial(n), frac_[:], ALU.add, ALU.mult)
            dve.drain()
            stt(exps[:], exps[:], 1.0, expo_i[:].bitcast(F32), ALU.add, ALU.mult)
            dve.drain()
            ear, dt = exps[:, 0:NST], exps[:, NST:]
            ts(adt[:], ear, dt, -1.0, ALU.mult, ALU.mult)
            ts(wdt[:], aim[:], dt, None, ALU.mult)
            dve.drain()

            def fraction(dst, src, times, t):
                ts(dst, src, times, None, ALU.mult)
                dve.drain()
                ts(t, dst, MAGIC, MAGIC, ALU.add, ALU.subtract)
                dve.drain()
                return tt(dst, dst, t, ALU.subtract)

            fraction(fr[:], wdt[:], 1.0 / TAU, tmp[:])
            dve.drain()
            fraction(fr2[:], wdt[:], 0.5 / TAU, tmp[:]).then_inc(angles_ok, 1)

            for n in range(4):
                dve.wait_ge(ld_q0[n], 16)
                words = raw0[:, 2 * n:2 * n + 2, :].rearrange("p t (g k) -> p t k g", k=3)
                dst = codes_i[:, 2 * n:2 * n + 2]
                ts(dst[:, :, 0, :], words[:, :, 0, :], 63, None, ALU.bitwise_and)
                ts(dst[:, :, 1, :], words[:, :, 0, :], 6, 63, ALU.logical_shift_right, ALU.bitwise_and)
                ts(dst[:, :, 2, :], words[:, :, 1, :], 63, None, ALU.bitwise_and)
                ts(dst[:, :, 3, :], words[:, :, 2, :], 63, None, ALU.bitwise_and).then_inc(code_un, 1)

            for n in range(4):
                dve.wait_ge(qt_mm, 2 * n + 2)
                v.tensor_copy(q_t[:, :, (2 * n + 1) * P:(2 * n + 2) * P],
                              banks(4).rearrange("p (k n) -> p k n", n=P)).then_inc(qt_ev[1], 2)

            dve.wait_ge(consts, 2)
            dve.wait_ge(ld_small, 16 * (4 + GH))
            v.tensor_copy(len_pf[:], len_p[:])
            tt(mask_t[:], mask_t[:].bitcast(I32), len_bc[:].unsqueeze(1).to_broadcast([P, BLK, B]), ALU.is_lt)
            for k in range(4):
                ts(code_mask[:, k:k + 1], chan[:], k, 1, ALU.logical_shift_right, ALU.bitwise_and)
            dve.drain()
            ts(code_mask[:], code_mask[:], -1.0, None, ALU.add)
            dve.wait_ge(ld_bc, 48)
            ts(nzs_bc[:], nzs_bc[:], 32.0, -1.0, ALU.subtract, ALU.mult)
            dve.drain()
            tt(nzs_bc[:], nzs_bc[:], scale_bc[:], ALU.mult).then_inc(nzs_ok, 1)
            dve.wait_ge(kp_dma, 16)
            dve.wait_ge(qt_mm, 8)
            dve.drain()

            def coefficients():
                dve.wait_ge(exps_ok, 1)
                stt(em1[:], ea[:], 1.0, th[:], ALU.add, ALU.mult)
                stt(cm1[:], sh[:], -2.0, sh[:], ALU.mult, ALU.mult)
                tt(zi[:], ea[:], sn[:], ALU.mult)
                dve.drain()
                stt(cs1[:], cm1[:], 1.0, em1[:], ALU.add, ALU.mult)
                dve.drain()
                tt(zr[:], cs1[:], cm1[:], ALU.add)
                dve.drain()
                cr, ci = natc[:, :, 0], natc[:, :, 1]

                def combine(dst, p0, q0_, p1, q1_, op):
                    tt(tmp[:], p0, q0_, ALU.mult)
                    tt(tmp2[:], p1, q1_, ALU.mult)
                    dve.drain()
                    tt(dst, tmp[:], tmp2[:], op)
                    dve.drain()

                combine(nr_[:], cr, zr[:], ci, zi[:], ALU.subtract)
                combine(ni_[:], cr, zi[:], ci, zr[:], ALU.add)
                combine(m2[:], ear, ear, aim[:], aim[:], ALU.add)
                v.reciprocal(m2[:], m2[:])
                combine(csr[:], ni_[:], aim[:], nr_[:], ear, ALU.subtract)
                combine(csi[:], ni_[:], ear, nr_[:], aim[:], ALU.add)
                alpha, beta, damp, freq = nat2
                stt(alpha[:, 0:NST], csr[:], 2.0, m2[:], ALU.mult, ALU.mult)
                stt(alpha[:, NST:], csi[:], 2.0, m2[:], ALU.mult, ALU.mult)
                stt(beta[:, 0:NST], csi[:], 2.0, m2[:], ALU.mult, ALU.mult)
                stt(beta[:, NST:], csr[:], -2.0, m2[:], ALU.mult, ALU.mult)
                v.tensor_copy(damp[:, 0:NST], adt[:])
                v.tensor_copy(damp[:, NST:], adt[:])
                ts(freq[:, 0:NST], wdt[:], 1.0 / TAU, None, ALU.mult)
                ts(freq[:, NST:], wdt[:], 1.0 / TAU, None, ALU.mult).then_inc(param_ok, 1)
            def copy_parameters():
                dve.wait_ge(k_mm, 1)
                for n in range(4):
                    last = v.tensor_copy(par[n][:], ps[:, 7, n * C:(n + 1) * C])
                last.then_inc(par_ok, 1)

            def low_part(r, u):
                dve.wait_ge(h_hi, r + 1)
                wait_pos(dve, zero_ok, r - 1)
                v.tensor_copy(s_sb[:, u:u + 1], ps[:, 6, 0:1])
                tt(ht[u][1][:].rearrange("p k r -> p (k r)"), banks(0),
                   ht[u][0][:].rearrange("p k r -> p (k r)").bitcast(F32), ALU.subtract).then_inc(h_lo, 1)

            def layer0(r, u, i):
                if not is_int(r) or r < NR - 1:
                    low_part(r + 1, 1 - u)
                if is_int(r) and r == 0:
                    copy_parameters()
                if u == 1:
                    if is_int(i) and i == 0:
                        dve.wait_ge(lut_mm, 3)
                    kernel_phases(i)
                if not is_int(r) or r > 0:
                    store_x1t(r - 1)
                if u == 1:
                    kernel_turns(i)
                elif not (is_int(i) and i == 0):
                    kernel_factors(i - 1)
                dve.drain()
                dve.wait_ge(main0, r + 1)
                tt(prod[:], banks(2 + 2 * u), scale_bc[:], ALU.mult)
                dve.drain()
                dve.wait_ge(xb_ok, r + 1)
                wait_pos(dve, x1_tr, r - 1)
                if not is_int(r) or r >= 2:
                    dve.wait_ge(st_x1[u], 8 * (r - u))
                tt(x1[u][:], prod[:], xb[u][:], ALU.add).then_inc(x1_ok, 1)

            def over_m(t, j):
                return t[:, ds(KH * j, KH)].unsqueeze(2).to_broadcast([P, KH, 32])

            m_row = iota_m[:].unsqueeze(1).to_broadcast([P, KH, 32])

            def kernel_phases(j):
                dve.drain()
                tt(waves[:, 2], over_m(par[3], j), m_row, ALU.mult)
                dve.drain()
                ts(waves[:, 0], waves[:, 2], 32.0, 0.25, ALU.mult, ALU.add)
                ts(waves[:, 1], waves[:, 2], 32.0, None, ALU.mult)
                dve.drain()
                ts(waves[:, 2], waves[:, 2], shift[:], None, ALU.add)

            def kernel_turns(j):
                dve.drain()
                ts(damps[:], waves[:], MAGIC, MAGIC, ALU.add, ALU.subtract)
                dve.drain()
                tt(waves[:], waves[:], damps[:], ALU.subtract)
                dve.drain()
                tt(damps[:, 2], over_m(par[2], j), m_row, ALU.mult).then_inc(phase_ok, 1)

            def kernel_factors(j):
                dve.drain()
                dve.wait_ge(wave_ok, j + 1)
                dve.wait_ge(k_mm, j + 1)
                tt(waves[:, 0], waves[:, 0], over_m(par[0], j), ALU.mult)
                tt(waves[:, 1], waves[:, 1], over_m(par[1], j), ALU.mult)
                tt(e_short[:], waves[:, 2], damps[:, 1], ALU.mult)
                v.tensor_copy(d_now[:], d_sb[:, ds(KH * j, KH)])
                dve.drain()
                tt(waves[:, 0], waves[:, 0], waves[:, 1], ALU.add)
                dve.drain()
                tt(e_long[:, :, ::-1], waves[:, 0], damps[:, 0], ALU.mult).then_inc(e_ok, 1)

            def store_x1t(r):
                dve.wait_ge(x1_tr, r + 1)
                for b2 in range(2):
                    dst = x1t[:, :, :, ds(2 * r + b2, 1)].rearrange("p h k a -> p k (h a)")
                    src = banks(6).rearrange("p (k b h) -> p k b h", b=2, h=C)[:, :, b2, :]
                    last = tt(dst, src, mask_t[:, :, ds(2 * r + b2, 1)].to_broadcast([P, BLK, C]), ALU.mult)
                last.then_inc(x1t_ok, 1)

            low_part(0, 0)
            coefficients()
            pairs(dve, NR, layer0)
            store_x1t(NR - 1)
            kernel_factors(NR // 2 - 1)

            def rows(g, u):
                dve.drain()
                dve.wait_ge(row_tr, g + 1)
                wait_pos(dve, norm_ok, g - 1)
                if not is_int(g) or g >= 2:
                    dve.wait_ge(st_xc[u], 32 * (g - u))
                tt(xr[u][:].rearrange("p (j k w) -> p k w j", k=BLK, j=16),
                   banks(4).rearrange("p (k t) -> p k t", t=P)[:, :, ::-1].rearrange("p k (w j) -> p k w j", j=16),
                   mask_row[:].rearrange("p (k w j) -> p k w j", k=BLK, j=16), ALU.mult).then_inc(xr_ok, 1)

            def unpack(dst, src):
                for j in range(16):
                    if j < 15:
                        last = ts(dst(j), src, 14 - j, 0x4000, ALU.logical_shift_left, ALU.bitwise_and)
                    else:
                        last = ts(dst(j), src, 1, 0x4000, ALU.logical_shift_right, ALU.bitwise_and)
                return last

            def plane_bits(i):
                dve.wait_ge(ld_words, 16 * (i + 1))
                wait_pos(dve, code_mm, i)
                bv = bits[:].bitcast(U16).rearrange("p k (j w) -> p k j w", j=16)
                unpack(lambda j: bv[:, :, j, :], plane_words[:].bitcast(U16)).then_inc(words_read, 1)
                dve.drain()
                stt(bits[:, 0::2, :], bits[:, 1::2, :], 2.0, bits[:, 0::2, :], ALU.mult, ALU.add)
                dve.drain()
                stt(bits[:, 0, :], bits[:, 2, :], 4.0, bits[:, 0, :], ALU.mult, ALU.add).then_inc(bits_ok, 1)

            def pack_onehot(i):
                dve.wait_ge(ld_rep, 128 * (i + 1))
                dst = packed[:, ds(i * 512, 512)]
                ts(dst, rep_words[:, 0, :], code_mask[:, 0:1], None, ALU.bitwise_xor)
                for k in range(1, 4):
                    dve.drain()
                    last = stt(dst, rep_words[:, k, :], code_mask[:, k:k + 1], dst, ALU.bitwise_xor, ALU.bitwise_and)
                last.then_inc(pack_ok, 1)

            def select_masks(i):
                dve.wait_ge(code_ok, i + 1)
                main = sel[:, 0:NCH * MC].rearrange("p (c t l k o) -> p c t l k o", t=KT, l=4, k=CG, o=8)
                tail = sel[:, NCH * MC:NCH * MC + KT * 4 * LAST * 8].rearrange("p (t l k o) -> p t l k o", t=KT, l=4, k=LAST)
                for l in range(4):
                    ts(main[:, :, :, l, :, ds(i, 1)].rearrange("p c t k a -> p t c (k a)"),
                       code8[:, :, 0:NCH * CG].rearrange("p t (c k) -> p t c k", k=CG), 8 >> l, None, ALU.bitwise_and)
                    last = ts(tail[:, :, l, :, ds(i, 1)].rearrange("p t k a -> p t (k a)"),
                              code8[:, :, NCH * CG:], 8 >> l, None, ALU.bitwise_and)
                last.then_inc(sel_ok, 1)

            dve.wait_ge(consts, 3)
            ts(mask_row[:], mask_row[:].bitcast(I32), len_pf[:], None, ALU.is_lt)
            def one_hot(c, t, n):
                src = packed[:].bitcast(U16).rearrange("p (g w) -> p g w", w=64)[:, ds(CG * c, n), :]
                dst = onehot[t // 4][:].bitcast(U16)
                for j in (2 * t, 2 * t + 1):
                    o = dst[:, 0:n, j % 8, :]
                    if j < 15:
                        last = ts(o, src, 14 - j, 0x4000, ALU.logical_shift_left, ALU.bitwise_and)
                    else:
                        last = ts(o, src, 1, 0x4000, ALU.logical_shift_right, ALU.bitwise_and)
                last.then_inc(oh_ok, 1)

            for u in range(2):
                dve.wait_ge(st_x1[u], 8 * NR)
            dve.drain()
            plane_bits(0)
            pack_onehot(0)
            rows(0, 0)
            select_masks(0)

            def two_groups(i):
                if is_int(i) and i == 7:
                    pack_onehot(i)
                    rows(2 * i - 1, 1)
                else:
                    rows(2 * i - 1, 1)
                    pack_onehot(i)
                plane_bits(i)
                rows(2 * i, 0)
                if is_int(i) and i == 7:
                    dve.wait_ge(conv_mm, C - GH)
                    for t in range(4):
                        one_hot(0, t, CG)
                    rows(NGH - 1, 1)
                select_masks(i)

            two_groups(1)
            with dve.Fori(2, 7) as i:
                two_groups(i)
            two_groups(7)

            def pick(c, t, n):
                u, per = t % 2, n // 4
                dve.wait_ge(leaves, KT * c + t + 1)
                dve.wait_ge(mask_cp, KT * c + t + 1)
                v.memset(gate[:], 0.0)
                view = ps[:, 4 * u:4 * u + 4, 0:per * 8 * LW].rearrange("p a (k l) -> p a k l", l=LW)
                flat = leaf_mask[u][:].rearrange("p l k a -> p (l k a)")
                for l in range(4):
                    w = 8 >> l
                    mk = flat[:, l * n * 8:(l + 1) * n * 8].rearrange("p (a k) -> p a k", a=4).unsqueeze(3)
                    last = v.copy_predicated(view[:, :, :, 0:w], mk.to_broadcast([P, 4, per * 8, w]), view[:, :, :, w:2 * w])
                    if l < 3:
                        dve.drain()
                last.then_inc(picked, 1)

            use8, ahead, t0, t1_, slot_l, pos, dif, _ = sm

            def count_rows():
                dve.wait_ge(norm_ok, NGH)
                dve.wait_ge(consts, 4)
                ts(use8[:], norm2[:], THR, None, ALU.is_gt)
                v.memset(ahead[:, 0:1], 0.0)
                dve.drain()
                v.tensor_copy(ahead[:, 1:], use8[:, :NGH - 1])
                dve.drain()
                cur, other = ahead, t0
                for s in (1, 2, 4, 8):
                    v.tensor_copy(other[:, 0:s], cur[:, 0:s])
                    tt(other[:, s:], cur[:, s:], cur[:, :NGH - s], ALU.add)
                    dve.drain()
                    cur, other = other, cur
                assert cur is ahead
                tt(sc[0][:], ahead[:, NGH - 1:], use8[:, NGH - 1:], ALU.add).then_inc(rank, 1)
            def place_rows():
                dve.wait_ge(leaves, 4)
                v.tensor_copy(pos[:], ranks)
                ts(si[0][:], total8, float(P - 1), None, ALU.add).then_inc(rank, 1)
                dve.drain()
                ts(si[1][:], si[0][:], 7, 7, ALU.logical_shift_right, ALU.logical_shift_left)
                dve.drain()
                v.tensor_copy(sc[1][:], si[1][:])
                tt(slot_l[:], elem_f[:], pos[:], ALU.subtract)
                dve.drain()
                ts(slot_l[:], slot_l[:], sc[1][:], None, ALU.add)
                dve.drain()
                tt(dif[:], pos[:], slot_l[:], ALU.subtract)
                dve.drain()
                tt(dif[:], dif[:], use8[:], ALU.mult)
                dve.drain()
                tt(slots[:], dif[:], slot_l[:], ALU.add).then_inc(rank, 1)
                ts(table_off[:], tile_at[:], sc[1][0:1, :], float(KT * O), ALU.is_ge, ALU.mult)

            def chunk(c, n, n_next):
                for t in range(KT):
                    if is_int(c) and c == 0 and t == 3:
                        place_rows()
                    pick(c, t, n)
                    if is_int(c) and c == 0 and t == 1:
                        count_rows()
                    if n_next:
                        one_hot(c + 1, t, n_next)

            dve.drain()
            dve.wait_ge(conv_mm, C)
            for t in range(4, KT):
                one_hot(0, t, CG)
            chunk(0, CG, CG)
            with dve.Fori(1, NCH - 1) as c:
                chunk(c, CG, CG)
            dve.wait_ge(ids_ld, 16)
            ts(gather_id[:], ids_sb[:], float(ROWS - 1), None, ALU.min).then_inc(rank, 1)
            chunk(NCH - 1, CG, LAST)
            chunk(NCH, LAST, 0)

            def x_low(k, u):
                dve.wait_ge(x_hi_ok, k + 1)
                wait_pos(dve, main1, k - 1)
                tt(x_lo[u][:], banks(0), x_hi[u][:].bitcast(F32), ALU.subtract).then_inc(x_lo_ok, 1)

            def result(k, u):
                dve.wait_ge(main1, k + 1)
                dve.wait_ge(res_ok, k + 1)
                if not is_int(k) or k >= 2:
                    dve.wait_ge(st_out[u], 8 * (k - u))
                tt(yo[u][:], banks(2 + 2 * u), x1g[u][:], ALU.add).then_inc(yo_ok, 1)

            x_low(0, 0)
            for t in range(KT):
                dve.wait_ge(w8_hi_ok, t + 1)
                tt(w_lo[:, 0, t, :], w1[:, 0, t, :], w_hi[:, 0, t, :].bitcast(F32), ALU.subtract).then_inc(w8_lo_ok, 1)
            dve.wait_ge(w4_hi_ok, KT)
            tt(w_lo[:, 1, KT - 1, :], w1[:, 1, KT - 1, :], w_hi[:, 1, KT - 1, :].bitcast(F32),
               ALU.subtract).then_inc(w8_lo_ok, 1)
            x_low(1, 1)
            result(0, 0)
            x_low(2, 0)
            result(1, 1)
            with dve.Fori(1, NR // 2) as i:
                x_low(2 * i + 1, 1)
                result(2 * i, 0)
                x_low(2 * i + 2, 0)
                result(2 * i + 1, 1)
            result(TILES - 1, 0)


_INS = ['x', 'itok_B_0_15', 'itok_B_8_3872', 'L0_cond_weights', 'L0_ffn_qweight', 'L0_ffn_weight_scale',
        'L0_ffn_weight_zero_point', 'L0_ffn_bias', 'L1_cond_log_dt', 'L1_cond_C', 'L1_cond_log_A_real',
        'L1_cond_A_imag', 'L1_cond_D', 'L1_ffn_qweight', 'L1_ffn_lut4', 'L1_ffn_lut8', 'L1_ffn_bias']
_OUTS = [((32, 64, 1024), 'float32')]


def kernel(**inputs):
    import numpy as _np
    import concourse.bacc as _bacc
    from concourse import mybir as _mybir
    from concourse.bass_utils import run_bass_kernel_spmd as _run

    nc = _bacc.Bacc("TRN2", target_bir_lowering=False, num_devices=1)
    arrays, args = {}, []
    for name in _INS:
        a = _np.ascontiguousarray(inputs[name])
        arrays[f"in_{name}_dram"] = a
        args.append(nc.dram_tensor(f"in_{name}_dram", a.shape, _mybir.dt.from_np(a.dtype), kind="ExternalInput").ap())
    for i, (shape, dtype) in enumerate(_OUTS):
        dt = _mybir.dt.from_np(_np.dtype(dtype))
        args.append(nc.dram_tensor(f"out_{i}_dram", shape, dt, kind="ExternalOutput").ap())
    adaln_ffn_kernel(nc, *args)
    r = _run(nc, [arrays], core_ids=[0])
    return r.results[0]["out_0_dram"]
```
